# Optimizing a Trainium2 kernel written in Bass

```python
import numpy as np
import jax
import jax.numpy as jnp

def _softmax(x, axis=-1):
    return jax.nn.softmax(x, axis=axis)

def _gelu(x):
    return jax.nn.gelu(x, approximate=True)

def _silu(x):
    return jax.nn.silu(x)

def _sigmoid(x):
    return jax.nn.sigmoid(x)

def _layernorm(x, axis=-1, eps=1e-05):
    m = jnp.mean(x, axis=axis, keepdims=True)
    v = jnp.var(x, axis=axis, keepdims=True)
    return (x - m) / jnp.sqrt(v + eps)

def _scatter_add(tgt, idx, src, axis=0):
    return tgt.at[idx].add(src)

def _segment_sum(src, seg, n):
    return jax.ops.segment_sum(src, seg, n)
kernel_name = 'mk_macaron_d1_jaxref_r8_3fba7e'

def setup_inputs(seed: int=0):
    np.random.seed(seed)
    _w = jnp.asarray

    def _L0_attn_setup():
        import jax, jax.numpy as jnp
        import numpy as np
        H = 16
        W = 64
        NEG = -1000000000.0

        def _neighborhood(t, nb):
            tp = jnp.pad(t, ((0, 0), (W, W), (0, 0), (0, 0)))
            idx = jnp.arange(nb)[:, None] * W + jnp.arange(3 * W)[None, :]
            return tp[:, idx]
        key = jax.random.key(seed)
        k0, k1, k2 = jax.random.split(key, 3)
        B, N, C = (2, 512, 128)
        x = jax.random.normal(k0, (B, N, C), dtype=jnp.float32)
        w_qkv = jax.random.normal(k1, (C, 3 * C), dtype=jnp.float32) * 0.02
        w_out = jax.random.normal(k2, (C, C), dtype=jnp.float32) * 0.02
        b_out = jnp.zeros((C,), dtype=jnp.float32)
        return {'x': x, 'w_qkv': w_qkv, 'w_out': w_out, 'b_out': b_out}
    _L0_attn_in = _L0_attn_setup()

    def _L0_ffn_setup():
        import jax, jax.numpy as jnp
        import numpy as np
        H = 128
        E = 8
        B, S = (4, 256)
        key = jax.random.key(seed)
        k1, k2, k3, k4 = jax.random.split(key, 4)
        x = jax.random.normal(k1, (B, S, H), dtype=jnp.float32)
        wg = jax.random.normal(k2, (H, E), dtype=jnp.float32) * 0.02
        W = jax.random.normal(k3, (E, H, H), dtype=jnp.float32) * 0.02
        b = jax.random.normal(k4, (E, H), dtype=jnp.float32) * 0.02
        return {'x': x, 'wg': wg, 'W': W, 'b': b}
    _L0_ffn_in = _L0_ffn_setup()
    _d = {'L0_attn_x': _L0_attn_in['x'], 'L0_attn_w_qkv': _L0_attn_in['w_qkv'], 'L0_attn_w_out': _L0_attn_in['w_out'], 'L0_attn_b_out': _L0_attn_in['b_out'], 'L0_ffn_wg': _L0_ffn_in['wg'], 'L0_ffn_W': _L0_ffn_in['W'], 'L0_ffn_b': _L0_ffn_in['b']}
    _x0 = _d['L0_attn_x']
    _d['L0_attn_x'] = jax.random.normal(jax.random.fold_in(jax.random.key(seed), 1), (8, 512, 128), dtype=_x0.dtype)
    del _x0
    return _d

def reference(L0_attn_x, L0_attn_w_qkv, L0_attn_w_out, L0_attn_b_out, L0_ffn_wg, L0_ffn_W, L0_ffn_b):

    def _L0_attn_ref(x, w_qkv, w_out, b_out):
        import jax, jax.numpy as jnp
        import numpy as np
        H = 16
        W = 64
        NEG = -1000000000.0

        def _neighborhood(t, nb):
            tp = jnp.pad(t, ((0, 0), (W, W), (0, 0), (0, 0)))
            idx = jnp.arange(nb)[:, None] * W + jnp.arange(3 * W)[None, :]
            return tp[:, idx]
        B, N, C = x.shape
        Dh = C // H
        scale = Dh ** (-0.5)
        pad = W // 2
        nb = N // W
        qkv = (x @ w_qkv).reshape(B, N, 3, H, Dh)
        q, k, v = (qkv[:, :, 0], qkv[:, :, 1], qkv[:, :, 2])
        qb = q.reshape(B, nb, W, H, Dh)
        kn = _neighborhood(k, nb)
        vn = _neighborhood(v, nb)
        logits = jnp.einsum('bnqhd,bnkhd->bhnqk', qb, kn) * scale
        q_idx = jnp.arange(W)[:, None]
        k_idx = jnp.arange(3 * W)[None, :]
        rel = k_idx - W - q_idx
        win = (rel >= -pad) & (rel <= pad - 1)
        j_abs = jnp.arange(nb)[:, None, None] * W + (k_idx[None] - W)
        valid = win[None] & (j_abs >= 0) & (j_abs < N)
        logits = jnp.where(valid[None, None], logits, NEG)
        attn_local = jax.nn.softmax(logits, axis=-1)
        out_local = jnp.einsum('bhnqk,bnkhd->bnqhd', attn_local, vn).reshape(B, N, H, Dh)
        kg = k[:, ::W]
        vg = v[:, ::W]
        lg = jnp.einsum('bnhd,bghd->bhng', q, kg) * scale
        attn_g = jax.nn.softmax(lg, axis=-1)
        out_global = jnp.einsum('bhng,bghd->bnhd', attn_g, vg)
        out = (out_local + out_global).reshape(B, N, C)
        return out @ w_out + b_out

    def _L0_ffn_ref(x, wg, W, b):
        import jax, jax.numpy as jnp
        import numpy as np
        H = 128
        E = 8
        B, S = (4, 256)
        Bb, Ss, Hh = x.shape
        Ee = wg.shape[1]
        T = Bb * Ss
        C = T // Ee
        xt = x.reshape(T, Hh)
        logits = xt @ wg
        probs = jax.nn.softmax(logits, axis=-1)
        idx = jnp.argmax(probs, axis=-1)
        mask = jax.nn.one_hot(idx, Ee, dtype=xt.dtype)
        locations = jnp.cumsum(mask, axis=0) - mask
        mask = mask * (locations < C).astype(xt.dtype)
        gate = jnp.sum(probs * mask, axis=-1)
        loc_s = jnp.sum(locations * mask, axis=-1).astype(jnp.int32)
        loc_oh = jax.nn.one_hot(loc_s, C, dtype=xt.dtype)
        dispatch = mask[:, :, None] * loc_oh[:, None, :]
        combine = gate[:, None, None] * dispatch
        exp_in = jnp.einsum('tec,th->ech', dispatch, xt)
        exp_out = jnp.einsum('ech,efh->ecf', exp_in, W) + b[:, None, :]
        out = jnp.einsum('tec,ecf->tf', combine, exp_out)
        return out.reshape(Bb, Ss, Hh)
    x = L0_attn_x
    x = x + 0.5 * _L0_ffn_ref(_layernorm(x, axis=-1), L0_ffn_wg, L0_ffn_W, L0_ffn_b)
    x = x + _L0_attn_ref(_layernorm(x, axis=-1), L0_attn_w_qkv, L0_attn_w_out, L0_attn_b_out)
    x = x + 0.5 * _L0_ffn_ref(_layernorm(x, axis=-1), L0_ffn_wg, L0_ffn_W, L0_ffn_b)
    return x

_drawn_inputs = setup_inputs


def setup_inputs(seed=0):
    import zlib

    import numpy as np

    out = dict(_drawn_inputs(seed))
    spreads = {'L0_attn_b_out': (0.0, 0.1)}
    factors = {'L0_attn_w_qkv': 2.951, 'L0_attn_w_out': 2.901, 'L0_ffn_b': 8.0}
    for name, (base, spread) in spreads.items():
        noise = np.random.default_rng([zlib.crc32(name.encode()), seed]).standard_normal(out[name].shape)
        drawn = base * np.exp(spread * noise) if base else spread * noise
        out[name] = jnp.asarray(drawn.astype(out[name].dtype))
    for name, factor in factors.items():
        out[name] = (out[name] * factor).astype(out[name].dtype)
    return out
```

```python
from contextlib import ExitStack

import concourse.bass as bass
from concourse import mybir

F32 = mybir.dt.float32
F16 = mybir.dt.float16
BF16 = mybir.dt.bfloat16
I32 = mybir.dt.int32
ALU = mybir.AluOpType
ACT = mybir.ActivationFunctionType
AX = mybir.AxisListType

P = 128
NB = 8
SEQ = 512
TILES = SEQ // P
E = 8
CAP = NB * SEQ // E
H = 16
DH = P // H
W = 64
BLOCKS = SEQ // W
HALO = W // 2
G = SEQ // W
C4 = H // 4
SCALE = float(DH) ** -0.5
EPS = 1e-5
NEG = -1.0e9
VW = DH + 1

IDENT = 0
TRI = IDENT + P
ONES = TRI + P
MASKS = ONES + P
HEADS = MASKS + 3 * W
FIRST = HEADS + H
NCONST = FIRST + E

FFN_T = ["xt", "gate", "loc", "gmt", "bias"]


def bank_uses():
    t, y0, y1, s = [], [], [], []
    o = []
    order = schedule()
    for what in order:
        kind, n = what
        if kind == "a_xt":
            t.append("a_xt")
        elif kind in ("a_gate", "a_loc", "a_gmt", "a_bias", "b_xt", "b_gate", "b_loc", "b_gmt", "b_bias", "a_nt", "a_lg", "a_pgt", "a_vg"):
            t.append(kind)
        elif kind in ("a_exp", "b_exp"):
            y0.append(f"{kind}{n}")
            y1.append(f"{kind}{n}")
        elif kind == "a_qk":
            y0.append("a_q")
            y1.append("a_k")
        elif kind == "a_v":
            y0.append("a_v0")
            y1.append("a_v1")
        elif kind in ("a_s", "b_s"):
            s.append(f"{kind}{n}")
        elif kind == "a_mt":
            o.append(f"a_mt{n}")
        elif kind == "b_pv" and n % 2 == 0:
            o.append(f"b_o{n // 2}")
        elif kind == "b_ot":
            t.append(f"b_ot{n}")
        elif kind == "b_og":
            y0.append(f"b_og{n}")
        elif kind == "b_bt":
            y1.append(f"b_bt{n}")
        elif kind == "b_wo":
            y0.append(f"b_wo{n}")
    return {"T": t, "Y0": y0, "Y1": y1, "S0": s[0::2], "S1": s[1::2], "O": o}


def schedule():
    out = [("a_xt", 0), ("a_gate", 0)]
    for n in range(BLOCKS):
        out.append(("b_s", n))
        if n == 0:
            out += [("a_exp", 0), ("a_loc", 0)]
        if n >= 1:
            out.append(("b_pv", n - 1))
        if n == 1:
            out += [("a_gmt", 0), ("a_bias", 0)]
        if n in (1, 2, 3):
            out.append(("a_exp", n))
        if n == 3:
            out += [("b_ot", 0), ("b_og", 0)]
        if n == 4:
            out += [("b_bt", 0), ("b_wo", 0)]
        if n == 5:
            out += [("b_ot", 1), ("b_og", 1)]
        if n == 6:
            out += [("b_bt", 1), ("b_wo", 1), ("a_nt", 0)]
        if n == 7:
            out += [("b_ot", 2), ("b_og", 2), ("b_bt", 2), ("b_wo", 2)]
    out += [("b_pv", 7), ("a_qk", 0), ("b_ot", 3), ("b_og", 3), ("a_vx", 0), ("b_bt", 3), ("b_wo", 3), ("a_v", 0)]
    out += [("a_lg", 0), ("a_s", 0), ("b_xt", 0), ("a_s", 1), ("a_pgt", 0), ("b_gate", 0), ("a_s", 2), ("b_exp", 0), ("a_s", 3), ("b_loc", 0),
            ("a_mt", 0), ("a_s", 4), ("b_gmt", 0), ("b_bias", 0), ("a_s", 5), ("a_vg", 0), ("b_exp", 1), ("a_s", 6), ("a_s", 7), ("b_exp", 2), ("a_mt", 1), ("b_exp", 3)]
    return [x for x in out if x[0] != "a_vx"]


def build(nc, x, w_q, w_k, w_v, w_out, b_out, w_gate, w_exp, b_exp, const, out):
    x_v = x.rearrange("b (t p) c -> b p t c", p=P)
    out_v = out.rearrange("b (t p) c -> b p t c", p=P)
    uses = bank_uses()

    with ExitStack() as ctx:
        def sb(name, shape, dt=F32):
            return ctx.enter_context(nc.sbuf_tensor(name, shape, dt))

        def sem(name):
            return ctx.enter_context(nc.semaphore(name))

        q_dram = nc.dram_tensor("q_parts", (P, 2, SEQ), F16).ap()
        k_dram = nc.dram_tensor("k_parts", (P, 2, SEQ + 2 * HALO), F16).ap()
        m_dram = nc.dram_tensor("max_parts", (H, 2, 8, 32), F16).ap()

        wq_s, wk_s, wv_s, wo_s = (sb(n, [P, P]) for n in ("wq_s", "wk_s", "wv_s", "wo_s"))
        bout_s = sb("bout_s", [P, P])
        wg_s = sb("wg_s", [P, E])
        we_s = sb("we_s", [P, E * P])
        bexp_s = sb("bexp_s", [TILES * E, TILES * P])
        cst = sb("cst", [P, NCONST])
        ident = cst[:, IDENT:IDENT + P]
        heads = cst[:, HEADS:HEADS + H]
        first = cst[:, FIRST:FIRST + E]
        identb = sb("identb", [P, P], BF16)
        trib = sb("trib", [P, P], BF16)
        onesb = sb("onesb", [P, P], BF16)
        masksb = sb("masksb", [P, 3, W], BF16)
        mhalf = sb("mhalf", [P, TILES])
        carry = [sb(f"carry{f}", [P, E]) for f in range(2)]

        x0 = sb("x0", [P, TILES, P])
        x1 = sb("x1", [P, TILES, P])
        x2 = sb("x2", [P, TILES, P])
        y = sb("y", [P, TILES, P])
        st = [sb(f"st{f}", [P, TILES, 6]) for f in range(3)]
        mv = [sb(f"mv{f}", [P, TILES, 2]) for f in range(3)]
        ve = [sb(f"ve{f}", [P, TILES]) for f in range(3)]
        rstd = [sb(f"rstd{f}", [P, TILES]) for f in range(3)]
        xn = [sb(f"xn{f}", [P, TILES, P]) for f in range(3)]
        xt = [sb(f"xt{f}", [P, SEQ]) for f in range(2)]
        lmax = [sb(f"lmax{f}", [P, TILES]) for f in range(2)]
        lsub = [sb(f"lsub{f}", [P, TILES, E]) for f in range(2)]
        lexp = [sb(f"lexp{f}", [P, TILES, E]) for f in range(2)]
        lsum = [sb(f"lsum{f}", [P, TILES]) for f in range(2)]
        prob = [sb(f"prob{f}", [P, TILES]) for f in range(2)]
        top = [sb(f"top{f}", [P, TILES, E]) for f in range(2)]
        topm = [sb(f"topm{f}", [P, TILES]) for f in range(2)]
        hot = [sb(f"hot{f}", [P, TILES, E]) for f in range(2)]
        hotb = [sb(f"hotb{f}", [P, TILES, E], BF16) for f in range(2)]
        loc = [sb(f"loc{f}", [P, TILES, E]) for f in range(2)]
        gm = [sb(f"gm{f}", [P, TILES, E]) for f in range(2)]
        gmt = [sb(f"gmt{f}", [TILES * E, P]) for f in range(2)]
        acc = [sb(f"acc{f}", [P, TILES, P]) for f in range(2)]

        nt = sb("nt", [P, SEQ + 2 * HALO])
        qf = sb("qf", [P, SEQ])
        kf = sb("kf", [P, SEQ])
        qhl = sb("qhl", [P, 2, SEQ], F16)
        khl = sb("khl", [P, 2, SEQ + 2 * HALO], F16)
        kge = sb("kge", [P, H, G])
        xgr = sb("xgr", [P, H, G])
        lgm = sb("lgm", [P, TILES * H])
        lgs = sb("lgs", [P, TILES * H, G])
        lge = sb("lge", [P, TILES * H, G])
        lgr = sb("lgr", [P, TILES * H])
        lgi = sb("lgi", [P, TILES * H])
        pg = sb("pg", [P, TILES * H, G])
        rmax = sb("rmax", [P, 2, H, 4, 2])
        nmax = sb("nmax", [P, 2, 32], F16)
        qx = [sb(f"qx{i}", [P, C4, 4, SEQ], F16) for i in range(2)]
        ks = [sb(f"ks{i}", [P, C4, SEQ + 2 * HALO], F16) for i in range(2)]
        va = [sb(f"va{i}", [P, BLOCKS, H, VW]) for i in range(2)]
        pgt = [sb(f"pgt{i}", [P, SEQ]) for i in range(2)]
        vge = [sb(f"vge{i}", [P, H, DH]) for i in range(2)]
        x1b = [sb(f"x1b{i}", [P, TILES, P]) for i in range(2)]
        pr = [sb(f"pr{i}", [P, H, W]) for i in range(2)]
        osb = [sb(f"osb{i}", [P, SEQ]) for i in range(2)]
        rl = [sb(f"rl{i}", [P, H]) for i in range(2)]
        ol = [sb(f"ol{i}", [P, H, DH]) for i in range(2)]
        og = [sb(f"og{i}", [P, P]) for i in range(2)]
        bt = [sb(f"bt{i}", [P, P]) for i in range(2)]

        bank = {n: ctx.enter_context(nc.psum_tensor(f"bank_{n}", [P, 512], F32)) for n in ("T", "Y0", "Y1", "O")}
        for n in ("S0", "S1"):
            bank[n] = ctx.enter_context(nc.psum_tensor(f"bank_{n}", [P, 1024], F32))
        T, Y0, Y1, O = bank["T"], bank["Y0"], bank["Y1"], bank["O"]
        S = [bank["S0"], bank["S1"]]
        full = {n: sem(f"bank_full_{n}") for n in bank}
        free = {n: sem(f"bank_free_{n}") for n in bank}

        per = {}
        sems = {}

        def signal(name, count):
            per[name] = count
            sems[name] = sem(name)

        consts_loaded, consts_ready, zeros_ready, stored = (sem(n) for n in ("consts_loaded", "consts_ready", "zeros_ready", "stored"))
        for f in range(2):
            signal(f"xt_ready{f}", 1)
            signal(f"lsub_ready{f}", 1)
            signal(f"lexp_ready{f}", 1)
            signal(f"hot_ready{f}", 1)
            signal(f"gm_ready{f}", 1)
            signal(f"gmt_ready{f}", 1)
        for f in range(3):
            signal(f"var_ready{f}", 1)
            signal(f"rstd_ready{f}", 1)
            signal(f"xn_ready{f}", TILES)
        signal("x_loaded", 16)
        signal("x1_ready", TILES)
        signal("x1b_ready", 1)
        signal("nt_ready", 1)
        signal("qf_ready", 1)
        signal("kf_ready", 1)
        signal("qk_hi_ready", 2)
        signal("qk_lo_ready", 2)
        signal("qk_in_dram", 2 * 16)
        signal("max_in_dram", 2 * 16)
        signal("k_stacked", 3 * 16)
        signal("q_spread", 12 * 16)
        signal("v_ready", 2)
        signal("kge_ready", 1)
        signal("xgr_ready", 1)
        signal("lgs_ready", 1)
        signal("lge_ready", 1)
        signal("pg_ready", 1)
        signal("pgt_ready", 1)
        signal("vge_ready", 1)
        signal("rmax_ready", BLOCKS)
        signal("nmax_ready", 2)
        signal("max_placed", 4 * 16)
        signal("p_ready", BLOCKS)
        signal("p_used", BLOCKS)
        signal("osb_ready", TILES)
        signal("og_ready", TILES)
        signal("bt_ready", TILES)
        signal("x2_ready", TILES)
        signal("y_ready", TILES)
        signal("dve_a", DVE_STEPS_A)
        signal("dve_b", DVE_STEPS_B)
        round_done = sem("round_done")

        only = {"a": {n: [u for u in uses[n] if u[0] == "a"] for n in uses},
                "b": {n: [u for u in uses[n] if u[0] == "b"] for n in uses},
                "ab": uses}

        class Round:

            def __init__(self, stages, i, parity):
                self.stages, self.i, self.parity = stages, i, parity
                self.steps = {"a": 0, "b": 0}

            def seq(self, stage):
                return self.i if stage == "a" else self.i - 1

            def buf(self, stage):
                return self.parity if stage == "a" else 1 - self.parity

            def uses_before(self, n):
                if self.stages == "a":
                    return 0
                return len(only["a"][n]) + (self.i - 1) * len(uses[n])

        def wait(eng, r, name, k, stage):
            eng.wait_ge(sems[name], r.seq(stage) * per[name] + k)
            if eng is nc.sync:
                eng.nop(nofuse=True)

        def wait_full(eng, r, n, use):
            eng.wait_ge(full[n], r.uses_before(n) + only[r.stages][n].index(use) + 1)

        def wait_free(eng, r, n, use):
            eng.wait_ge(free[n], r.uses_before(n) + only[r.stages][n].index(use) + 1)

        def rounds(eng, body):
            body(Round("a", 0, 0))
            with eng.Fori(0, (NB - 1) // 2) as k:
                body(Round("ab", 2 * k + 1, 1))
                body(Round("ab", 2 * k + 2, 0))
            body(Round("ab", NB - 1, 1))
            body(Round("b", NB, 0))

        def end_round(eng, r, last):
            last.then_inc(round_done, 1)
            eng.wait_ge(round_done, 5 * (r.i + 1))
            if eng is nc.sync:
                eng.nop(nofuse=True)

        block = ctx.enter_context(nc.Block())

        @block.sync
        def _(sp):
            for dst, src in ((cst[:, :], const), (wg_s[:, :], w_gate), (we_s[:, :], w_exp), (wq_s[:, :], w_q), (wk_s[:, :], w_k),
                             (wv_s[:, :], w_v), (wo_s[:, :], w_out), (bout_s[:, :], b_out)):
                sp.dma_start(dst, src).then_inc(consts_loaded, 16)
            sp.wait_ge(zeros_ready, 1)
            for t in range(TILES):
                sp.dma_start(bexp_s[t * E:(t + 1) * E, t * P:(t + 1) * P], b_exp).then_inc(consts_loaded, 16)

            def body(r):
                if "a" in r.stages:
                    i, pa = r.i, r.buf("a")
                    sp.dma_start(x0[:, :, :], x_v[i] if type(i) is int else x_v[bass.ds(i, 1)].rearrange("b p t c -> p (b t) c")).then_inc(sems["x_loaded"], 16)
                    wait(sp, r, "qk_hi_ready", 2, "a")
                    wait(sp, r, "qk_lo_ready", 2, "a")
                    sp.dma_start(q_dram, qhl[:, :, :]).then_inc(sems["qk_in_dram"], 16)
                    sp.dma_start(k_dram, khl[:, :, :]).then_inc(sems["qk_in_dram"], 16)
                    wait(sp, r, "qk_in_dram", 2 * 16, "a")
                    for term, part in enumerate((0, 0, 1)):
                        sp.dma_start(ks[pa][32 * term:32 * term + 32, :, :], k_dram[:, part, :].rearrange("(c p) w -> p c w", c=C4))\
                            .then_inc(sems["k_stacked"], 16)
                    for term, part in enumerate((0, 1, 0)):
                        for j in range(4):
                            sp.dma_start(qx[pa][32 * term + DH * j:32 * term + DH * (j + 1), :, j, :],
                                         q_dram[:, part, :].rearrange("(c j d) w -> j d c w", c=C4, j=4)[j]).then_inc(sems["q_spread"], 16)
                    for half in range(2):
                        wait(sp, r, "nmax_ready", half + 1, "a")
                        sp.dma_start(m_dram[:, half, :, :].rearrange("h u q -> h u q"), nmax[:, half, :]).then_inc(sems["max_in_dram"], 16)
                    wait(sp, r, "max_in_dram", 2 * 16, "a")
                    for j in range(4):
                        sp.dma_start(qx[pa][96 + j:97 + j, :, j, :], m_dram.rearrange("(c j) a u q -> j c (a u q)", j=4)[j].unsqueeze(0))\
                            .then_inc(sems["max_placed"], 16)
                if "b" in r.stages:
                    wait(sp, r, "y_ready", TILES, "b")
                    i = r.i - 1
                    sp.dma_start(out_v[i] if type(i) is int else out_v[bass.ds(i, 1)].rearrange("b p t c -> p (b t) c"), y[:, :, :]).then_inc(stored, 16)
                    sp.wait_ge(stored, 16 * r.i)
                    sp.nop(nofuse=True)
                if "a" in r.stages:
                    wait(sp, r, "max_placed", 4 * 16, "a")
                end_round(sp, r, sp.nop())

            rounds(sp, body)

        @block.gpsimd
        def _(pool):
            nc.gpsimd.memset(mhalf[:, :], -0.5).then_inc(consts_ready, 1)
            for i in range(2):
                nc.gpsimd.memset(va[i][:, :, :, :], 1.0).then_inc(consts_ready, 1)
            pool.wait_ge(consts_ready, NCONSTS_READY)

            def rsqrt(r, f, stage):
                wait(pool, r, f"var_ready{f}", 1, stage)
                nc.gpsimd.tensor_tensor(rstd[f][:, :], ve[f][:, :], mhalf[:, :], ALU.pow).then_inc(sems[f"rstd_ready{f}"], 1)

            def body(r):
                if "a" in r.stages:
                    rsqrt(r, 0, "a")
                    rsqrt(r, 1, "a")
                    wait(pool, r, "x1_ready", TILES, "a")
                    nc.gpsimd.tensor_tensor(x1b[r.buf("a")][:, :, :], x1[:, :, :], bout_s[:, :].unsqueeze(1).broadcast_to([P, TILES, P]),
                                            ALU.add).then_inc(sems["x1b_ready"], 1)
                if "b" in r.stages:
                    rsqrt(r, 2, "b")
                end_round(pool, r, pool.nop())

            rounds(pool, body)

        @block.tensor
        def _(pe):
            pe.wait_ge(consts_ready, NCONSTS_READY)

            def transposes(r, f, use, stage):
                wait_free(pe, r, "T", use)
                for t in range(TILES):
                    wait(pe, r, f"xn_ready{f}", t + 1, stage)
                    last = nc.tensor.transpose(T[:, t * P:(t + 1) * P], xn[f][:, t, :], ident)
                last.then_inc(full["T"], 1)

            def gate(r, f, stage):
                wait(pe, r, f"xt_ready{f}", 1, stage)
                wait_free(pe, r, "T", stage + "_gate")
                for t in range(TILES):
                    last = nc.tensor.matmul(T[:, t * E:(t + 1) * E], xt[f][:, t * P:(t + 1) * P], wg_s[:, :], start=True, stop=True,
                                            skip_group_check=True)
                last.then_inc(full["T"], 1)

            def locations(r, f, stage):
                wait(pe, r, f"hot_ready{f}", 1, stage)
                wait_free(pe, r, "T", stage + "_loc")
                hb = hotb[f][:, :, :].rearrange("p t e -> p (t e)")
                n = TILES * E
                nc.tensor.matmul(T[:, 0:n], trib[:, :], hb, start=True, stop=False, skip_group_check=True)
                for t in range(1, TILES):
                    nc.tensor.matmul(T[:, t * E:n], onesb[:, :], hb[:, 0:n - t * E], start=False, stop=False, skip_group_check=True)
                for t in range(TILES):
                    last = nc.tensor.matmul(T[:, n:n + E], onesb[:, :], hb[:, t * E:(t + 1) * E], start=False, stop=(t == TILES - 1),
                                            skip_group_check=True)
                last.then_inc(full["T"], 1)

            def gates_turned(r, f, stage):
                wait(pe, r, f"gm_ready{f}", 1, stage)
                wait_free(pe, r, "T", stage + "_gmt")
                nc.tensor.transpose(T[0:TILES * E, 0:P], gm[f][:, :, :].rearrange("p t e -> p (t e)"), ident).then_inc(full["T"], 1)

            def bias(r, f, stage):
                wait(pe, r, f"gmt_ready{f}", 1, stage)
                wait_free(pe, r, "T", stage + "_bias")
                nc.tensor.matmul(T[:, :], gmt[f][:, :], bexp_s[:, :], start=True, stop=True, skip_group_check=True).then_inc(full["T"], 1)

            def experts(r, f, stage, t):
                wait(pe, r, f"xt_ready{f}", 1, stage)
                for n in range(2):
                    wait_free(pe, r, f"Y{n}", f"{stage}_exp{t}")
                    nc.tensor.matmul(bank[f"Y{n}"][:, :], xt[f][:, t * P:(t + 1) * P], we_s[:, n * 512:(n + 1) * 512], start=True,
                                     stop=True, skip_group_check=True).then_inc(full[f"Y{n}"], 1)

            def q_k(r):
                wait(pe, r, "nt_ready", 1, "a")
                for n, w in (("Y0", wq_s), ("Y1", wk_s)):
                    wait_free(pe, r, n, {"Y0": "a_q", "Y1": "a_k"}[n])
                    nc.tensor.matmul(bank[n][:, :], w[:, :], nt[:, HALO:HALO + SEQ], start=True, stop=True,
                                     skip_group_check=True).then_inc(full[n], 1)

            def values(r):
                for n in range(2):
                    wait_free(pe, r, f"Y{n}", f"a_v{n}")
                    for m in range(4):
                        at = (4 * n + m) * W
                        last = nc.tensor.matmul(bank[f"Y{n}"][:, m * P:(m + 1) * P], nt[:, at:at + P], wv_s[:, :], start=True, stop=True,
                                                skip_group_check=True)
                    last.then_inc(full[f"Y{n}"], 1)

            def global_logits(r):
                wait(pe, r, "kge_ready", 1, "a")
                wait(pe, r, "qf_ready", 1, "a")
                wait_free(pe, r, "T", "a_lg")
                for t in range(TILES):
                    last = nc.tensor.matmul(T[:, t * P:(t + 1) * P], qf[:, t * P:(t + 1) * P], kge[:, :, :].rearrange("p h g -> p (h g)"),
                                            start=True, stop=True, skip_group_check=True)
                last.then_inc(full["T"], 1)

            def global_turned(r):
                wait(pe, r, "pg_ready", 1, "a")
                wait_free(pe, r, "T", "a_pgt")
                for t in range(TILES):
                    last = nc.tensor.transpose(T[:, t * P:(t + 1) * P], pg[:, t * H:(t + 1) * H, :].rearrange("p h g -> p (h g)"), ident)
                last.then_inc(full["T"], 1)

            def global_values(r):
                wait(pe, r, "xgr_ready", 1, "a")
                wait_free(pe, r, "T", "a_vg")
                nc.tensor.matmul(T[:, 0:P], xgr[:, :, :].rearrange("p h g -> p (h g)"), wv_s[:, :], start=True, stop=True,
                                 skip_group_check=True).then_inc(full["T"], 1)

            def logits(r, stage, n):
                s = f"S{n % 2}"
                pb = r.buf(stage)
                if n == 0:
                    if stage == "a":
                        wait(pe, r, "k_stacked", 3 * 16, "a")
                        wait(pe, r, "q_spread", 12 * 16, "a")
                wait_free(pe, r, s, f"{stage}_s{n}")
                mask = masksb[:, 1 if n == 0 else 2 if n == BLOCKS - 1 else 0, :].unsqueeze(1).broadcast_to([P, 8, W])
                for half in range(2):
                    dst = bank[s][:, half * 512:(half + 1) * 512]
                    nc.tensor.matmul(dst, identb[:, :], mask, start=True, stop=False, skip_group_check=True)
                    for c in (2 * half, 2 * half + 1):
                        rows = 96 if stage == "a" else P
                        last = nc.tensor.matmul(dst[:, (c % 2) * 256:(c % 2 + 1) * 256], ks[pb][0:rows, c, n * W:n * W + P],
                                                qx[pb][0:rows, c, :, n * W:(n + 1) * W], start=False, stop=True, skip_group_check=True)
                last.then_inc(full[s], 1)

            def maxima_turned(r, half):
                wait(pe, r, "rmax_ready", 4 * half + 4, "a")
                wait_free(pe, r, "O", f"a_mt{half}")
                nc.tensor.transpose(O[:, 0:P], rmax[:, half, :, :, :].rearrange("p h n v -> p (h n v)"), ident).then_inc(full["O"], 1)

            def weigh(r, n):
                pb = r.buf("b")
                wait(pe, r, "p_ready", n + 1, "b")
                if n % 2 == 0:
                    wait_free(pe, r, "O", f"b_o{n // 2}")
                for h in range(H):
                    j, c = h // 4, h % 4
                    last = nc.tensor.matmul(O[32 * c:32 * c + VW, j * P + (n % 2) * W:j * P + (n % 2 + 1) * W], va[pb][:, n, h, :],
                                            pr[n % 2][:, h, :], start=True, stop=True, skip_group_check=True)
                last.then_inc(sems["p_used"], 1)
                if n % 2 == 1:
                    pe.wait_ge(sems["p_used"], r.seq("b") * per["p_used"] + n + 1)
                    pe.nop().then_inc(full["O"], 1)

            def weighed_turned(r, t):
                wait(pe, r, "osb_ready", t + 1, "b")
                wait_free(pe, r, "T", f"b_ot{t}")
                for j in range(4):
                    last = nc.tensor.transpose(T[:, j * P:(j + 1) * P], osb[t % 2][:, j * P:(j + 1) * P], ident)
                last.then_inc(full["T"], 1)

            def global_out(r, t):
                wait_free(pe, r, "Y0", f"b_og{t}")
                pb = r.buf("b")
                nc.tensor.matmul(Y0[:, 0:P], pgt[pb][:, t * P:(t + 1) * P], vge[pb][:, :, :].rearrange("p h d -> p (h d)"), start=True,
                                 stop=True, skip_group_check=True).then_inc(full["Y0"], 1)

            def out_turned(r, t):
                wait(pe, r, "og_ready", t + 1, "b")
                wait_free(pe, r, "Y1", f"b_bt{t}")
                nc.tensor.transpose(Y1[:, 0:P], og[t % 2][:, :], ident).then_inc(full["Y1"], 1)

            def project(r, t):
                wait(pe, r, "bt_ready", t + 1, "b")
                wait_free(pe, r, "Y0", f"b_wo{t}")
                nc.tensor.matmul(Y0[:, 0:P], bt[t % 2][:, :], wo_s[:, :], start=True, stop=True, skip_group_check=True)\
                    .then_inc(full["Y0"], 1)

            def body(r):
                steps = {
                    "a_xt": lambda n: transposes(r, 0, "a_xt", "a"), "a_gate": lambda n: gate(r, 0, "a"),
                    "a_loc": lambda n: locations(r, 0, "a"), "a_gmt": lambda n: gates_turned(r, 0, "a"),
                    "a_bias": lambda n: bias(r, 0, "a"), "a_exp": lambda n: experts(r, 0, "a", n),
                    "a_nt": lambda n: transposes(r, 1, "a_nt", "a"), "a_qk": lambda n: q_k(r), "a_v": lambda n: values(r),
                    "a_lg": lambda n: global_logits(r), "a_pgt": lambda n: global_turned(r), "a_vg": lambda n: global_values(r),
                    "a_s": lambda n: logits(r, "a", n), "a_mt": lambda n: maxima_turned(r, n),
                    "b_s": lambda n: logits(r, "b", n), "b_pv": lambda n: weigh(r, n), "b_ot": lambda n: weighed_turned(r, n),
                    "b_og": lambda n: global_out(r, n), "b_bt": lambda n: out_turned(r, n), "b_wo": lambda n: project(r, n),
                    "b_xt": lambda n: transposes(r, 2, "b_xt", "b"), "b_gate": lambda n: gate(r, 1, "b"),
                    "b_loc": lambda n: locations(r, 1, "b"), "b_gmt": lambda n: gates_turned(r, 1, "b"),
                    "b_bias": lambda n: bias(r, 1, "b"), "b_exp": lambda n: experts(r, 1, "b", n),
                }
                for kind, n in schedule():
                    if kind[0] in r.stages:
                        steps[kind](n)
                end_round(pe, r, pe.nop())

            rounds(pe, body)

        @block.scalar
        def _(act):
            def copy_xt(r, f, stage):
                wait_full(act, r, "T", f"{stage}_xt")
                nc.scalar.activation(xt[f][:, :], T[:, :], ACT.Copy).then_inc(free["T"], 1)
                act.wait_ge(free["T"], r.uses_before("T") + only[r.stages]["T"].index(f"{stage}_xt") + 2)
                act.nop().then_inc(sems[f"xt_ready{f}"], 1)

            def gate_exp(r, f, stage):
                wait(act, r, f"lsub_ready{f}", 1, stage)
                nc.scalar.activation(lexp[f][:, :, :], lsub[f][:, :, :], ACT.Exp).then_inc(sems[f"lexp_ready{f}"], 1)

            def evacuate(r, n, use, dst, src, done, scale=1.0):
                wait_full(act, r, n, use)
                nc.scalar.activation(dst, src, ACT.Copy, scale=scale).then_inc(free[n], 1)
                act.wait_ge(free[n], r.uses_before(n) + only[r.stages][n].index(use) + 2)
                if done is not None:
                    act.nop().then_inc(sems[done], 1)

            def exponentials(r, n):
                wait_full(act, r, f"S{n % 2}", f"b_s{n}")
                if n >= 2:
                    wait(act, r, "p_used", n - 1, "b")
                evacuate_exp = nc.scalar.activation(pr[n % 2][:, :, :].rearrange("p h w -> p (h w)"), S[n % 2][:, :], ACT.Exp)
                evacuate_exp.then_inc(free[f"S{n % 2}"], 1)
                act.wait_ge(free[f"S{n % 2}"], r.uses_before(f"S{n % 2}") + only[r.stages][f"S{n % 2}"].index(f"b_s{n}") + 2)
                act.nop().then_inc(sems["p_ready"], 1)

            for i in range(2):
                pass
            act.wait_ge(consts_ready, NCONSTS_READY)

            def body(r):
                a, b = "a" in r.stages, "b" in r.stages
                pa = r.buf("a")
                if a:
                    copy_xt(r, 0, "a")
                    gate_exp(r, 0, "a")
                for n in range(BLOCKS):
                    if b:
                        exponentials(r, n)
                    if a and n == 1:
                        evacuate(r, "T", "a_gmt", gmt[0][:, :], T[0:TILES * E, 0:P], "gmt_ready0")
                    if b and n in (2, 4, 6):
                        t = n // 2 - 1
                        evacuate(r, "O", f"b_o{t}", osb[t % 2][:, :], O[:, :], "osb_ready")
                    if b and n in (4, 6):
                        t = n // 2 - 2
                        evacuate(r, "Y1", f"b_bt{t}", bt[t % 2][:, :], Y1[:, 0:P], "bt_ready")
                if a:
                    evacuate(r, "T", "a_nt", nt[:, HALO:HALO + SEQ], T[:, :], "nt_ready")
                if b:
                    evacuate(r, "Y1", "b_bt2", bt[0][:, :], Y1[:, 0:P], "bt_ready")
                    evacuate(r, "O", "b_o3", osb[1][:, :], O[:, :], "osb_ready")
                if a:
                    evacuate(r, "Y0", "a_q", qf[:, :], Y0[:, :], "qf_ready", scale=SCALE)
                    evacuate(r, "Y1", "a_k", kf[:, :], Y1[:, :], "kf_ready")
                    nc.scalar.activation(qhl[:, 0, :], qf[:, :], ACT.Copy).then_inc(sems["qk_hi_ready"], 1)
                    nc.scalar.activation(khl[:, 0, HALO:HALO + SEQ], kf[:, :], ACT.Copy).then_inc(sems["qk_hi_ready"], 1)
                    nc.scalar.activation(xgr[:, :, :], nt[:, HALO:HALO + SEQ:W].unsqueeze(1).broadcast_to([P, H, G]), ACT.Copy)\
                        .then_inc(sems["xgr_ready"], 1)
                if b:
                    evacuate(r, "Y1", "b_bt3", bt[1][:, :], Y1[:, 0:P], "bt_ready")
                if a:
                    for n in range(2):
                        evacuate(r, f"Y{n}", f"a_v{n}", va[pa][:, 4 * n:4 * n + 4, :, 0:DH],
                                 bank[f"Y{n}"][:, :].rearrange("p (n h d) -> p n h d", n=4, h=H), "v_ready")
                    wait(act, r, "lgs_ready", 1, "a")
                    nc.scalar.activation(lge[:, :, :], lgs[:, :, :], ACT.Exp).then_inc(sems["lge_ready"], 1)
                if b:
                    copy_xt(r, 1, "b")
                if a:
                    evacuate(r, "T", "a_pgt", pgt[pa][:, :], T[:, :], "pgt_ready")
                if b:
                    gate_exp(r, 1, "b")
                    evacuate(r, "T", "b_gmt", gmt[1][:, :], T[0:TILES * E, 0:P], "gmt_ready1")
                end_round(act, r, act.nop())

            rounds(act, body)

        @block.vector
        def _(dve):
            nc.vector.memset(bexp_s[:, :], 0.0).then_inc(zeros_ready, 1)
            for i in range(2):
                nc.vector.memset(qx[i][:, :, :, :], 0.0).then_inc(consts_ready, 1)
                nc.vector.memset(ks[i][0:96, :, :], 0.0).then_inc(consts_ready, 1)
                nc.vector.memset(ks[i][96:P, :, :], 1.0).then_inc(consts_ready, 1)
            nc.vector.memset(khl[:, :, :], 0.0).then_inc(consts_ready, 1)
            nc.vector.memset(nt[:, :], 0.0).then_inc(consts_ready, 1)
            nc.vector.memset(O[:, :], 0.0).then_inc(free["O"], 1)
            for f in range(2):
                nc.vector.memset(carry[f][:, :], 0.0).then_inc(consts_ready, 1)
            dve.wait_ge(consts_loaded, 12 * 16)
            nc.vector.tensor_copy(identb[:, :], cst[:, IDENT:IDENT + P]).then_inc(consts_ready, 1)
            nc.vector.tensor_copy(trib[:, :], cst[:, TRI:TRI + P]).then_inc(consts_ready, 1)
            nc.vector.tensor_copy(onesb[:, :], cst[:, ONES:ONES + P]).then_inc(consts_ready, 1)
            nc.vector.tensor_copy(masksb[:, :, :].rearrange("p m w -> p (m w)"), cst[:, MASKS:MASKS + 3 * W]).then_inc(consts_ready, 1)
            for n in ("T", "Y0", "Y1", "S0", "S1"):
                dve.nop().then_inc(free[n], 1)
            dve.wait_ge(consts_ready, NCONSTS_READY)

            def step(r, stage, ins):
                ins.then_inc(sems["dve_" + stage], 1)
                r.steps[stage] += 1
                wait(dve, r, "dve_" + stage, r.steps[stage], stage)

            def layernorm(r, f, stage, src):
                for t in range(TILES):
                    last = nc.vector.bn_stats(st[f][:, t, :], src[:, t, :])
                step(r, stage, last)
                dve.nop(nofuse=True)
                for t in range(TILES):
                    last = nc.vector.bn_aggr(mv[f][:, t, :], st[f][:, t, :])
                step(r, stage, last)
                nc.vector.tensor_scalar(ve[f][:, :], mv[f][:, :, 1], EPS, None, ALU.add).then_inc(sems[f"var_ready{f}"], 1)
                wait(dve, r, f"rstd_ready{f}", 1, stage)
                for t in range(TILES):
                    nc.vector.tensor_scalar(xn[f][:, t, :], src[:, t, :], mv[f][:, t, 0:1], rstd[f][:, t:t + 1], ALU.subtract, ALU.mult)\
                        .then_inc(sems[f"xn_ready{f}"], 1)

            def each(ap):
                return ap.unsqueeze(2).broadcast_to([P, TILES, E])

            def route(r, f, stage):
                g = T[:, 0:TILES * E].rearrange("p (t e) -> p t e", e=E)
                wait_full(dve, r, "T", f"{stage}_gate")
                step(r, stage, nc.vector.tensor_reduce(lmax[f][:, :], g, AX.X, ALU.max))
                nc.vector.tensor_tensor(lsub[f][:, :, :], g, each(lmax[f][:, :]), ALU.subtract).then_inc(free["T"], 1)
                dve.wait_ge(free["T"], r.uses_before("T") + only[r.stages]["T"].index(f"{stage}_gate") + 2)
                dve.nop().then_inc(sems[f"lsub_ready{f}"], 1)

            def choose(r, f, stage):
                wait(dve, r, f"lexp_ready{f}", 1, stage)
                step(r, stage, nc.vector.tensor_reduce(lsum[f][:, :], lexp[f][:, :, :], AX.X, ALU.add))
                step(r, stage, nc.vector.reciprocal(prob[f][:, :], lsum[f][:, :]))
                step(r, stage, nc.vector.scalar_tensor_tensor(out=top[f][:, :, :], in0=lexp[f][:, :, :], scalar=1.0,
                                                              in1=first.unsqueeze(1).broadcast_to([P, TILES, E]), op0=ALU.is_ge, op1=ALU.mult))
                step(r, stage, nc.vector.tensor_reduce(topm[f][:, :], top[f][:, :, :], AX.X, ALU.max))
                step(r, stage, nc.vector.tensor_tensor(hot[f][:, :, :], top[f][:, :, :], each(topm[f][:, :]), ALU.is_equal))
                nc.vector.tensor_copy(hotb[f][:, :, :], hot[f][:, :, :]).then_inc(sems[f"hot_ready{f}"], 1)

            def keep(r, f, stage):
                n = TILES * E
                wait_full(dve, r, "T", f"{stage}_loc")
                step(r, stage, nc.vector.tensor_tensor(loc[f][:, :, :], T[:, 0:n].rearrange("p (t e) -> p t e", e=E),
                                                       carry[f][:, :].unsqueeze(1).broadcast_to([P, TILES, E]), ALU.add))
                nc.vector.tensor_tensor(carry[f][:, :], carry[f][:, :], T[:, n:n + E], ALU.add).then_inc(free["T"], 1)
                step(r, stage, nc.vector.scalar_tensor_tensor(out=top[f][:, :, :], in0=loc[f][:, :, :], scalar=float(CAP), in1=hot[f][:, :, :],
                                                              op0=ALU.is_lt, op1=ALU.mult))
                nc.vector.scalar_tensor_tensor(out=gm[f][:, :, :], in0=top[f][:, :, :], scalar=0.5, in1=each(prob[f][:, :]),
                                               op0=ALU.mult, op1=ALU.mult).then_inc(sems[f"gm_ready{f}"], 1)

            def residual(r, f, stage, src):
                wait_full(dve, r, "T", f"{stage}_bias")
                nc.vector.tensor_tensor(acc[f][:, :, :], T[:, :].rearrange("p (t c) -> p t c", t=TILES), src, ALU.add).then_inc(free["T"], 1)
                dve.wait_ge(free["T"], r.uses_before("T") + only[r.stages]["T"].index(f"{stage}_bias") + 2)

            def combine(r, f, stage, t, dst, done):
                for e in range(E):
                    n = e // 4
                    if e % 4 == 0:
                        wait_full(dve, r, f"Y{n}", f"{stage}_exp{t}")
                    last = e == E - 1
                    ins = nc.vector.scalar_tensor_tensor(out=(dst if last else acc[f])[:, t, :], in0=bank[f"Y{n}"][:, (e % 4) * P:(e % 4 + 1) * P],
                                                         scalar=gm[f][:, t, e:e + 1], in1=acc[f][:, t, :], op0=ALU.mult, op1=ALU.add)
                    if e % 4 == 3:
                        ins.then_inc(free[f"Y{n}"], 1)
                        dve.wait_ge(free[f"Y{n}"], r.uses_before(f"Y{n}") + only[r.stages][f"Y{n}"].index(f"{stage}_exp{t}") + 2)
                    else:
                        step(r, stage, ins)
                dve.nop().then_inc(sems[done], 1)

            def lower_halves(r):
                wait(dve, r, "qk_hi_ready", 1, "a")
                nc.vector.tensor_tensor(qhl[:, 1, :], qf[:, :], qhl[:, 0, :], ALU.subtract).then_inc(sems["qk_lo_ready"], 1)
                wait(dve, r, "qk_hi_ready", 2, "a")
                nc.vector.tensor_tensor(khl[:, 1, HALO:HALO + SEQ], kf[:, :], khl[:, 0, HALO:HALO + SEQ], ALU.subtract)\
                    .then_inc(sems["qk_lo_ready"], 1)
                nc.vector.tensor_tensor(kge[:, :, :], heads.unsqueeze(2).broadcast_to([P, H, G]),
                                        kf[:, ::W].unsqueeze(1).broadcast_to([P, H, G]), ALU.mult).then_inc(sems["kge_ready"], 1)

            def all_g(ap):
                return ap.unsqueeze(2).broadcast_to([P, TILES * H, G])

            def global_shift(r):
                lg = T[:, :].rearrange("p (th g) -> p th g", g=G)
                wait_full(dve, r, "T", "a_lg")
                step(r, "a", nc.vector.tensor_reduce(lgm[:, :], lg, AX.X, ALU.max))
                nc.vector.tensor_tensor(lgs[:, :, :], lg, all_g(lgm[:, :]), ALU.subtract).then_inc(free["T"], 1)
                dve.wait_ge(free["T"], r.uses_before("T") + only[r.stages]["T"].index("a_lg") + 2)
                dve.nop().then_inc(sems["lgs_ready"], 1)

            def global_probs(r):
                wait(dve, r, "lge_ready", 1, "a")
                step(r, "a", nc.vector.tensor_reduce(lgr[:, :], lge[:, :, :], AX.X, ALU.add))
                step(r, "a", nc.vector.reciprocal(lgi[:, :], lgr[:, :]))
                nc.vector.tensor_tensor(pg[:, :, :], lge[:, :, :], all_g(lgi[:, :]), ALU.mult).then_inc(sems["pg_ready"], 1)

            def global_values(r):
                wait_full(dve, r, "T", "a_vg")
                nc.vector.tensor_tensor(vge[r.buf("a")][:, :, :], T[:, 0:P].rearrange("p (h d) -> p h d", d=DH),
                                        heads.unsqueeze(2).broadcast_to([P, H, DH]), ALU.mult).then_inc(free["T"], 1)

            def block_max(r, n):
                wait_full(dve, r, f"S{n % 2}", f"a_s{n}")
                nc.vector.tensor_reduce(rmax[:, n // 4, :, n % 4, :], S[n % 2][:, :].rearrange("p (h v q) -> p h v q", v=2, q=32), AX.X, ALU.max,
                                        apply_transpose=True).then_inc(free[f"S{n % 2}"], 1)
                dve.wait_ge(free[f"S{n % 2}"], r.uses_before(f"S{n % 2}") + only[r.stages][f"S{n % 2}"].index(f"a_s{n}") + 2)
                dve.nop().then_inc(sems["rmax_ready"], 1)

            def query_max(r, half):
                wait_full(dve, r, "O", f"a_mt{half}")
                nc.vector.tensor_reduce(nmax[:, half, :], O[:, 0:P].rearrange("p (k q) -> p q k", k=4), AX.X, ALU.max, negate=True)\
                    .then_inc(free["O"], 1)
                dve.wait_ge(free["O"], r.uses_before("O") + only[r.stages]["O"].index(f"a_mt{half}") + 2)
                dve.nop().then_inc(sems["nmax_ready"], 1)

            def normalise(r, t):
                wait_full(dve, r, "T", f"b_ot{t}")
                o = T[:, :].rearrange("p (h u) -> p h u", u=32)
                step(r, "b", nc.vector.reciprocal(rl[t % 2][:, :], o[:, :, DH]))
                nc.vector.tensor_tensor(ol[t % 2][:, :, :], o[:, :, 0:DH], rl[t % 2][:, :].unsqueeze(2).broadcast_to([P, H, DH]), ALU.mult)\
                    .then_inc(free["T"], 1)
                dve.wait_ge(free["T"], r.uses_before("T") + only[r.stages]["T"].index(f"b_ot{t}") + 2)
                wait_full(dve, r, "Y0", f"b_og{t}")
                nc.vector.tensor_tensor(og[t % 2][:, :], ol[t % 2][:, :, :].rearrange("p h d -> p (h d)"), Y0[:, 0:P], ALU.add)\
                    .then_inc(free["Y0"], 1)
                dve.wait_ge(free["Y0"], r.uses_before("Y0") + only[r.stages]["Y0"].index(f"b_og{t}") + 2)
                dve.nop().then_inc(sems["og_ready"], 1)

            def attention_out(r, t):
                wait_full(dve, r, "Y0", f"b_wo{t}")
                nc.vector.tensor_tensor(x2[:, t, :], Y0[:, 0:P], x1b[r.buf("b")][:, t, :], ALU.add).then_inc(free["Y0"], 1)
                dve.wait_ge(free["Y0"], r.uses_before("Y0") + only[r.stages]["Y0"].index(f"b_wo{t}") + 2)

            def body(r):
                a, b = "a" in r.stages, "b" in r.stages
                if a:
                    wait(dve, r, "x_loaded", 16, "a")
                    layernorm(r, 0, "a", x0)
                    route(r, 0, "a")
                    choose(r, 0, "a")
                    keep(r, 0, "a")
                    residual(r, 0, "a", x0[:, :, :])
                    for t in range(TILES):
                        combine(r, 0, "a", t, x1, "x1_ready")
                if b:
                    normalise(r, 0)
                    attention_out(r, 0)
                if a:
                    layernorm(r, 1, "a", x1)
                if b:
                    normalise(r, 1)
                    attention_out(r, 1)
                    normalise(r, 2)
                    attention_out(r, 2)
                if a:
                    lower_halves(r)
                if b:
                    normalise(r, 3)
                    attention_out(r, 3)
                    layernorm(r, 2, "b", x2)
                if a:
                    global_shift(r)
                    block_max(r, 0)
                    block_max(r, 1)
                    global_probs(r)
                if b:
                    route(r, 1, "b")
                if a:
                    block_max(r, 2)
                if b:
                    choose(r, 1, "b")
                if a:
                    block_max(r, 3)
                    query_max(r, 0)
                if b:
                    keep(r, 1, "b")
                if a:
                    block_max(r, 4)
                if b:
                    residual(r, 1, "b", x2[:, :, :])
                if a:
                    block_max(r, 5)
                    global_values(r)
                if b:
                    combine(r, 1, "b", 0, y, "y_ready")
                if a:
                    block_max(r, 6)
                if b:
                    combine(r, 1, "b", 1, y, "y_ready")
                if a:
                    block_max(r, 7)
                if b:
                    combine(r, 1, "b", 2, y, "y_ready")
                if a:
                    query_max(r, 1)
                if b:
                    combine(r, 1, "b", 3, y, "y_ready")
                for s, n in (("a", DVE_STEPS_A), ("b", DVE_STEPS_B)):
                    if s in r.stages:
                        assert r.steps[s] == n, (s, r.steps[s])
                end_round(dve, r, dve.nop())

            rounds(dve, body)


DVE_STEPS_A = 39
DVE_STEPS_B = 38
NCONSTS_READY = 3 + 14


def constants(np):
    c = np.zeros((P, NCONST), np.float32)
    k = np.arange(P)[:, None]
    c[:, IDENT:IDENT + P] = np.eye(P)
    c[:, TRI:TRI + P] = k < np.arange(P)[None]
    c[:, ONES:ONES + P] = 1.0
    band = (k >= np.arange(W)[None]) & (k - np.arange(W)[None] <= W - 1)
    inside = [k >= 0, k >= HALO, k < P - HALO]
    for m in range(3):
        c[:, MASKS + m * W:MASKS + (m + 1) * W] = np.where(band & inside[m], 0.0, NEG)
    c[:, HEADS:HEADS + H] = k // DH == np.arange(H)[None]
    c[:, FIRST:FIRST + E] = E - np.arange(E)
    return c


def kernel(**inputs):
    import numpy as np
    import concourse.bacc as bacc
    from concourse.bass_utils import run_bass_kernel_spmd

    a = {k: np.asarray(v) for k, v in inputs.items()}
    w_qkv = a["L0_attn_w_qkv"]
    arrays = {
        "x": a["L0_attn_x"],
        "w_q": w_qkv[:, 0:P], "w_k": w_qkv[:, P:2 * P], "w_v": w_qkv[:, 2 * P:3 * P],
        "w_out": a["L0_attn_w_out"],
        "b_out": np.broadcast_to(a["L0_attn_b_out"], (P, P)),
        "w_gate": a["L0_ffn_wg"],
        "w_exp": a["L0_ffn_W"].transpose(2, 0, 1).reshape(P, E * P),
        "b_exp": a["L0_ffn_b"],
        "const": constants(np),
    }
    nc = bacc.Bacc("TRN2", target_bir_lowering=False, num_devices=1)
    arrays = {f"in_{n}": np.ascontiguousarray(v) for n, v in arrays.items()}
    aps = [nc.dram_tensor(n, v.shape, mybir.dt.from_np(v.dtype), kind="ExternalInput").ap() for n, v in arrays.items()]
    out = nc.dram_tensor("out", (NB, SEQ, P), F32, kind="ExternalOutput").ap()
    build(nc, *aps, out)
    r = run_bass_kernel_spmd(nc, [arrays], core_ids=[0])
    return r.results[0]["out"]
```

```python
from contextlib import ExitStack

import concourse.bass as bass
from concourse import mybir

F32 = mybir.dt.float32
F16 = mybir.dt.float16
BF16 = mybir.dt.bfloat16
ALU = mybir.AluOpType
ACT = mybir.ActivationFunctionType
AX = mybir.AxisListType

P = 128
NB = 8
SEQ = 512
TILES = SEQ // P
E = 8
CAP = NB * SEQ // E
H = 16
DH = P // H
W = 64
BLOCKS = SEQ // W
HALO = W // 2
KEYS = SEQ + 2 * HALO
G = SEQ // W
C4 = H // 4
TERMS = 3
STACK = 4 * DH * TERMS
SCALE = float(DH) ** -0.5
EPS = 1e-5
NEG = -1.0e9
VW = DH + 1

IDENT = 0
TRI = IDENT + P
ONES = TRI + P
MASKS = ONES + P
HEADS = MASKS + 3 * W
FIRST = HEADS + H
NCONST = FIRST + E

USES = {
    "T": "b_nt a_xt a_gate a_loc b_lg a_gmt a_bias c_ot0 b_pgt b_vg c_ot1 c_ot2 c_ot3 d_xt d_gate d_loc d_gmt d_bias".split(),
    "Y0": "b_q b_v0 c_og0 c_wo0 a_exp0 c_og1 c_wo1 a_exp1 c_og2 c_wo2 c_og3 c_wo3 a_exp2 a_exp3 d_exp0 d_exp1 d_exp2 d_exp3".split(),
    "Y1": "b_k b_v1 c_bt0 a_exp0 c_bt1 a_exp1 c_bt2 c_bt3 a_exp2 a_exp3 d_exp0 d_exp1 d_exp2 d_exp3".split(),
    "O": "c_o0 c_o1 c_o2 c_o3 b_mt0 b_mt1".split(),
    "S0": "c_s0 c_s2 c_s4 c_s6 b_s0 b_s2 b_s4 b_s6".split(),
    "S1": "c_s1 c_s3 c_s5 c_s7 b_s1 b_s3 b_s5 b_s7".split(),
}


def build(nc, x, w_q, w_k, w_v, w_out, b_out, w_gate, w_exp, b_exp, const, out):
    x_v = x.rearrange("b (t p) c -> b p t c", p=P)
    out_v = out.rearrange("b (t p) c -> b p t c", p=P)

    with ExitStack() as ctx:
        def sb(name, shape, dt=F32):
            return ctx.enter_context(nc.sbuf_tensor(name, shape, dt))

        def sem(name):
            return ctx.enter_context(nc.semaphore(name))

        q_dram = nc.dram_tensor("q_parts", (P, TERMS, SEQ), F16).ap()
        k_dram = nc.dram_tensor("k_parts", (P, TERMS, KEYS), F16).ap()
        m_dram = nc.dram_tensor("max_parts", (H, 2, 8, 32), F16).ap()

        wq_s, wk_s, wv_s, wo_s = (sb(n, [P, P]) for n in ("wq_s", "wk_s", "wv_s", "wo_s"))
        bout_s = sb("bout_s", [P, P])
        wg_s = sb("wg_s", [P, E])
        we_s = sb("we_s", [P, E * P])
        bexp_s = sb("bexp_s", [TILES * E, TILES * P])
        cst = sb("cst", [P, NCONST])
        ident = cst[:, IDENT:IDENT + P]
        heads = cst[:, HEADS:HEADS + H]
        first = cst[:, FIRST:FIRST + E]
        identb = sb("identb", [P, P], BF16)
        trib = sb("trib", [P, P], BF16)
        onesb = sb("onesb", [P, P], BF16)
        masksb = sb("masksb", [P, 3, W], BF16)
        mhalf = sb("mhalf", [P, TILES])

        x0 = [sb(f"x0_{i}", [P, TILES, P]) for i in range(2)]
        x1 = [sb(f"x1_{i}", [P, TILES, P]) for i in range(2)]
        x2 = sb("x2", [P, TILES, P])
        y = sb("y", [P, TILES, P])
        st = [sb(f"st{f}", [P, TILES, 6]) for f in range(3)]
        mv = [sb(f"mv{f}", [P, TILES, 2]) for f in range(3)]
        ve = [sb(f"ve{f}", [P, TILES]) for f in range(3)]
        rstd = [sb(f"rstd{f}", [P, TILES]) for f in range(3)]
        shift = [sb(f"shift{f}", [P, TILES]) for f in range(3)]
        xn = [sb(f"xn{f}", [P, TILES, P]) for f in range(3)]
        carry = [sb(f"carry{f}", [P, E]) for f in range(2)]
        xt = [sb(f"xt{f}", [P, SEQ]) for f in range(2)]
        lmax = [sb(f"lmax{f}", [P, TILES]) for f in range(2)]
        lsub = [sb(f"lsub{f}", [P, TILES, E]) for f in range(2)]
        lexp = [sb(f"lexp{f}", [P, TILES, E]) for f in range(2)]
        lsum = [sb(f"lsum{f}", [P, TILES]) for f in range(2)]
        prob = [sb(f"prob{f}", [P, TILES]) for f in range(2)]
        top = [sb(f"top{f}", [P, TILES, E]) for f in range(2)]
        topm = [sb(f"topm{f}", [P, TILES]) for f in range(2)]
        hot = [sb(f"hot{f}", [P, TILES, E]) for f in range(2)]
        hotb = [sb(f"hotb{f}", [P, TILES, E], BF16) for f in range(2)]
        loc = [sb(f"loc{f}", [P, TILES, E]) for f in range(2)]
        gm = [sb(f"gm{f}", [P, TILES, E]) for f in range(2)]
        gmt = [sb(f"gmt{f}", [TILES * E, P]) for f in range(2)]
        acc = [sb(f"acc{f}", [P, TILES, P]) for f in range(2)]
        odd = [sb(f"odd{f}", [P, TILES, P]) for f in range(2)]

        nt = sb("nt", [P, KEYS])
        qf = sb("qf", [P, SEQ])
        kf = sb("kf", [P, SEQ])
        q3 = sb("q3", [P, TERMS, SEQ], F16)
        k3 = sb("k3", [P, TERMS, KEYS], F16)
        kge = sb("kge", [P, H, G])
        xgr = sb("xgr", [P, H, G])
        lgm = sb("lgm", [P, TILES * H])
        lgs = sb("lgs", [P, TILES * H, G])
        lge = sb("lge", [P, TILES * H, G])
        lgr = sb("lgr", [P, TILES * H])
        lgi = sb("lgi", [P, TILES * H])
        pg = sb("pg", [P, TILES * H, G])
        rmax = sb("rmax", [P, 2, H, 4, 2])
        nmax = sb("nmax", [P, 2, 32], F16)
        qx = [sb(f"qx{i}", [P, C4, 4, SEQ], F16) for i in range(2)]
        ks = [sb(f"ks{i}", [P, C4, KEYS], F16) for i in range(2)]
        va = [sb(f"va{i}", [P, BLOCKS, H, VW]) for i in range(2)]
        pgt = [sb(f"pgt{i}", [P, SEQ]) for i in range(2)]
        vge = [sb(f"vge{i}", [P, H, DH]) for i in range(2)]
        x1b = [sb(f"x1b{i}", [P, TILES, P]) for i in range(2)]
        pr = [sb(f"pr{i}", [P, H, W]) for i in range(2)]
        osb = [sb(f"osb{i}", [P, SEQ]) for i in range(2)]
        rl = [sb(f"rl{i}", [P, H]) for i in range(2)]
        ol = [sb(f"ol{i}", [P, H, DH]) for i in range(2)]
        og = [sb(f"og{i}", [P, P]) for i in range(2)]
        bt = [sb(f"bt{i}", [P, P]) for i in range(2)]

        bank = {n: ctx.enter_context(nc.psum_tensor(f"bank_{n}", [P, 512], F32)) for n in ("T", "Y0", "Y1", "O")}
        for n in ("S0", "S1"):
            bank[n] = ctx.enter_context(nc.psum_tensor(f"bank_{n}", [P, 1024], F32))
        T, Y0, Y1, O = bank["T"], bank["Y0"], bank["Y1"], bank["O"]
        full = {n: sem(f"bank_full_{n}") for n in bank if n != "O"}
        read = {n: sem(f"bank_read_{n}") for n in bank}
        s_bank = {u: n for n in ("S0", "S1") for u in USES[n]}

        per, sems = {}, {}

        def signal(name, count):
            per[name] = count
            sems[name] = sem(name)

        consts_loaded, consts_ready, zeros_ready = (sem(n) for n in ("consts_loaded", "consts_ready", "zeros_ready"))
        for f in range(2):
            signal(f"lexp_ready{f}", 1)
            signal(f"hot_ready{f}", 1)
            signal(f"gm_ready{f}", 1)
        for f in range(3):
            signal(f"var_ready{f}", 1)
            signal(f"rstd_ready{f}", 1)
            signal(f"shift_ready{f}", 1)
            signal(f"xn_ready{f}", TILES)
        signal("x_loaded", 16)
        signal("x1_ready", TILES)
        signal("x1b_ready", 1)
        signal("q_hi_ready", 1)
        signal("k_hi_ready", 1)
        signal("q_lo_ready", 1)
        signal("k_lo_ready", 1)
        signal("q_in_dram", 16)
        signal("k_in_dram", 16)
        signal("k_stacked", 16)
        signal("q_spread", 4 * 16)
        signal("max_in_dram", 2 * 16)
        signal("max_placed", 4 * 16)
        signal("max_turned", 2)
        signal("kge_ready", 1)
        signal("xgr_ready", 1)
        signal("lge_ready", 1)
        signal("pg_ready", 1)
        signal("weighed", BLOCKS)
        signal("og_ready", TILES)
        signal("y_ready", TILES)
        signal("stored", 16)
        steps = {s: sem(f"dve_steps_{s}") for s in "pabcd"}

        LAG = {"p": -1, "a": 0, "b": 1, "c": 2, "d": 2}

        class Round:

            def __init__(self, stages, i, parity):
                self.stages, self.i, self.parity = stages, i, parity
                self.steps = dict.fromkeys("pabcd", 0)
                self.claims = dict.fromkeys(USES, 0)
                self.order = {n: [u for u in USES[n] if u[0] in stages] for n in USES}

            def seq(self, stage):
                return self.i - LAG[stage]

            def buf(self, stage):
                return (self.parity + LAG[stage]) % 2

            def position(self, n, use):
                before = self.order[n].index(use)
                for s in "abcd":
                    count = sum(u[0] == s for u in USES[n])
                    before = before + count * (self.seq(s) if s in self.stages else min(max(self.seq(s), 0), NB))
                return before

            def nth(self, name, k, stage):
                return self.seq(stage) * per[name] + k

            def ran(self, stage, back=1):
                return type(self.i) is not int or self.seq(stage) >= back

            def last(self, name, stage, back=1):
                return (self.seq(stage) - back + 1) * per[name]

            def filled(self, n, use):
                return self.position(n, use) + 1

            def emptied(self, n, use):
                return self.position(n, use) + 2

            def claim(self, n, use):
                assert self.order[n][self.claims[n]] == use, (n, use, self.order[n][self.claims[n]])
                self.claims[n] += 1
                return self.position(n, use) + 1

            def step(self, stage, k):
                return self.seq(stage) * DVE_STEPS[stage] + k

            def mark(self, stage):
                self.steps[stage] += 1
                return self.steps[stage]

        def rounds(eng, body):
            body(Round("p", -1, 1))
            body(Round("pa", 0, 0))
            body(Round("pab", 1, 1))
            body(Round("pabcd", 2, 0))
            with eng.Fori(0, (NB - 4) // 2) as k:
                body(Round("pabcd", 2 * k + 3, 1))
                body(Round("pabcd", 2 * k + 4, 0))
            body(Round("abcd", NB - 1, 1))
            body(Round("bcd", NB, 0))
            body(Round("cd", NB + 1, 1))

        block = ctx.enter_context(nc.Block())

        @block.sync
        def _(sp):
            for dst, src in ((cst[:, :], const), (wg_s[:, :], w_gate), (we_s[:, :], w_exp), (wq_s[:, :], w_q), (wk_s[:, :], w_k),
                             (wv_s[:, :], w_v), (wo_s[:, :], w_out), (bout_s[:, :], b_out)):
                sp.dma_start(dst, src).then_inc(consts_loaded, 16)
            sp.wait_ge(zeros_ready, 1)
            for t in range(TILES):
                sp.dma_start(bexp_s[t * E:(t + 1) * E, t * P:(t + 1) * P], b_exp).then_inc(consts_loaded, 16)
            sp.wait_ge(consts_ready, NCONSTS_READY)

            def sequence(view, i):
                return view[i] if type(i) is int else view[bass.ds(i, 1)].rearrange("b p t c -> p (b t) c")

            def load(r):
                if r.ran("p"):
                    sp.wait_ge(sems["var_ready0"], r.last("var_ready0", "p"))
                    sp.nop(nofuse=True)
                if r.ran("p", 2):
                    sp.wait_ge(sems["x1_ready"], r.last("x1_ready", "p", 2))
                    sp.nop(nofuse=True)
                sp.dma_start(x0[r.buf("p")][:, :, :], sequence(x_v, r.seq("p"))).then_inc(sems["x_loaded"], 16)

            def stack(r):
                pb = r.buf("b")
                sp.wait_ge(sems["q_lo_ready"], r.nth("q_lo_ready", 1, "b"))
                sp.nop(nofuse=True)
                sp.dma_start(q_dram, q3[:, :, :]).then_inc(sems["q_in_dram"], 16)
                sp.wait_ge(sems["k_lo_ready"], r.nth("k_lo_ready", 1, "b"))
                sp.nop(nofuse=True)
                sp.dma_start(k_dram, k3[:, :, :]).then_inc(sems["k_in_dram"], 16)
                sp.wait_ge(sems["q_in_dram"], r.nth("q_in_dram", 16, "b"))
                sp.nop(nofuse=True)
                for j in range(4):
                    sp.dma_start(qx[pb][24 * j:24 * j + 24, :, j, :], q_dram.rearrange("(c j d) t w -> j (d t) c w", c=C4, j=4)[j])\
                        .then_inc(sems["q_spread"], 16)
                sp.wait_ge(sems["k_in_dram"], r.nth("k_in_dram", 16, "b"))
                sp.nop(nofuse=True)
                sp.dma_start(ks[pb][0:STACK, :, :], k_dram.rearrange("(c jd) t w -> (jd t) c w", c=C4)).then_inc(sems["k_stacked"], 16)

            def place_max(r):
                for half in range(2):
                    sp.wait_ge(read["O"], r.emptied("O", f"b_mt{half}"))
                    sp.nop(nofuse=True)
                    sp.dma_start(m_dram[:, half, :, :], nmax[:, half, :]).then_inc(sems["max_in_dram"], 16)
                sp.wait_ge(sems["max_in_dram"], r.nth("max_in_dram", 2 * 16, "b"))
                sp.nop(nofuse=True)
                for j in range(4):
                    sp.dma_start(qx[r.buf("b")][STACK + j:STACK + j + 1, :, j, :],
                                 m_dram.rearrange("(c j) a u q -> j c (a u q)", j=4)[j].unsqueeze(0)).then_inc(sems["max_placed"], 16)

            def store(r):
                sp.wait_ge(sems["y_ready"], r.nth("y_ready", TILES, "d"))
                sp.nop(nofuse=True)
                sp.dma_start(sequence(out_v, r.seq("d")), y[:, :, :]).then_inc(sems["stored"], 16)

            def body(r):
                if "p" in r.stages:
                    load(r)
                if "b" in r.stages:
                    stack(r)
                    place_max(r)
                if "d" in r.stages:
                    store(r)
                if "b" in r.stages:
                    sp.wait_ge(sems["max_placed"], r.nth("max_placed", 4 * 16, "b"))
                    sp.nop(nofuse=True)

            rounds(sp, body)
            sp.wait_ge(sems["stored"], 16 * NB)

        @block.gpsimd
        def _(pool):
            nc.gpsimd.memset(mhalf[:, :], -0.5).then_inc(consts_ready, 1)
            for i in range(2):
                nc.gpsimd.memset(va[i][:, :, :, :], 1.0).then_inc(consts_ready, 1)
            pool.wait_ge(consts_ready, NCONSTS_READY)

            def rsqrt(r, f, stage):
                pool.wait_ge(sems[f"var_ready{f}"], r.nth(f"var_ready{f}", 1, stage))
                nc.gpsimd.tensor_tensor(rstd[f][:, :], ve[f][:, :], mhalf[:, :], ALU.pow).then_inc(sems[f"rstd_ready{f}"], 1)

            def add_bias(r):
                pb = r.buf("b")
                pool.wait_ge(sems["x1_ready"], r.nth("x1_ready", TILES, "b"))
                nc.gpsimd.tensor_tensor(x1b[pb][:, :, :], x1[pb][:, :, :], bout_s[:, :].unsqueeze(1).broadcast_to([P, TILES, P]), ALU.add)\
                    .then_inc(sems["x1b_ready"], 1)

            def body(r):
                if "b" in r.stages:
                    add_bias(r)
                if "p" in r.stages:
                    rsqrt(r, 0, "p")
                if "d" in r.stages:
                    rsqrt(r, 2, "d")
                if "a" in r.stages:
                    rsqrt(r, 1, "a")

            rounds(pool, body)

        @block.tensor
        def _(pe):
            pe.wait_ge(consts_ready, NCONSTS_READY)
            pe.wait_ge(consts_loaded, 12 * 16)

            def turn(r, f, use, stage):
                pe.wait_ge(read["T"], r.claim("T", use))
                for t in range(TILES):
                    pe.wait_ge(sems[f"xn_ready{f}"], r.nth(f"xn_ready{f}", t + 1, stage))
                    last = nc.tensor.transpose(T[:, t * P:(t + 1) * P], xn[f][:, t, :], ident)
                last.then_inc(full["T"], 1)

            def gate(r, f, stage):
                pe.wait_ge(read["T"], r.emptied("T", stage + "_xt"))
                pe.wait_ge(read["T"], r.claim("T", stage + "_gate"))
                for t in range(TILES):
                    last = nc.tensor.matmul(T[:, t * E:(t + 1) * E], xt[f][:, t * P:(t + 1) * P], wg_s[:, :], start=True, stop=True,
                                            skip_group_check=True)
                last.then_inc(full["T"], 1)

            def locations(r, f, stage):
                pe.wait_ge(sems[f"hot_ready{f}"], r.nth(f"hot_ready{f}", 1, stage))
                pe.wait_ge(read["T"], r.claim("T", stage + "_loc"))
                hb = hotb[f][:, :, :].rearrange("p t e -> p (t e)")
                n = TILES * E
                nc.tensor.matmul(T[:, 0:n], trib[:, :], hb, start=True, stop=False, skip_group_check=True)
                for t in range(1, TILES):
                    nc.tensor.matmul(T[:, t * E:n], onesb[:, :], hb[:, 0:n - t * E], start=False, stop=False, skip_group_check=True)
                for t in range(TILES):
                    last = nc.tensor.matmul(T[:, n:n + E], onesb[:, :], hb[:, t * E:(t + 1) * E], start=False, stop=(t == TILES - 1),
                                            skip_group_check=True)
                last.then_inc(full["T"], 1)

            def gates_turned(r, f, stage):
                pe.wait_ge(sems[f"gm_ready{f}"], r.nth(f"gm_ready{f}", 1, stage))
                pe.wait_ge(read["T"], r.claim("T", stage + "_gmt"))
                nc.tensor.transpose(T[0:TILES * E, 0:P], gm[f][:, :, :].rearrange("p t e -> p (t e)"), ident).then_inc(full["T"], 1)

            def bias(r, f, stage):
                pe.wait_ge(read["T"], r.emptied("T", stage + "_gmt"))
                pe.wait_ge(read["T"], r.claim("T", stage + "_bias"))
                nc.tensor.matmul(T[:, :], gmt[f][:, :], bexp_s[:, :], start=True, stop=True, skip_group_check=True).then_inc(full["T"], 1)

            def experts(r, f, stage, t):
                for n in range(2):
                    pe.wait_ge(read[f"Y{n}"], r.claim(f"Y{n}", f"{stage}_exp{t}"))
                    nc.tensor.matmul(bank[f"Y{n}"][:, :], xt[f][:, t * P:(t + 1) * P], we_s[:, n * 512:(n + 1) * 512], start=True,
                                     stop=True, skip_group_check=True).then_inc(full[f"Y{n}"], 1)

            def q_k(r):
                pe.wait_ge(read["T"], r.emptied("T", "b_nt"))
                for n, w, use in (("Y0", wq_s, "b_q"), ("Y1", wk_s, "b_k")):
                    pe.wait_ge(read[n], r.claim(n, use))
                    nc.tensor.matmul(bank[n][:, :], w[:, :], nt[:, HALO:HALO + SEQ], start=True, stop=True,
                                     skip_group_check=True).then_inc(full[n], 1)

            def values(r):
                for n in range(2):
                    pe.wait_ge(read[f"Y{n}"], r.claim(f"Y{n}", f"b_v{n}"))
                    for m in range(4):
                        at = (4 * n + m) * W
                        last = nc.tensor.matmul(bank[f"Y{n}"][:, m * P:(m + 1) * P], nt[:, at:at + P], wv_s[:, :], start=True, stop=True,
                                                skip_group_check=True)
                    last.then_inc(full[f"Y{n}"], 1)

            def global_logits(r):
                pe.wait_ge(sems["kge_ready"], r.nth("kge_ready", 1, "b"))
                pe.wait_ge(read["T"], r.claim("T", "b_lg"))
                for t in range(TILES):
                    last = nc.tensor.matmul(T[:, t * P:(t + 1) * P], qf[:, t * P:(t + 1) * P], kge[:, :, :].rearrange("p h g -> p (h g)"),
                                            start=True, stop=True, skip_group_check=True)
                last.then_inc(full["T"], 1)

            def global_turned(r):
                pe.wait_ge(sems["pg_ready"], r.nth("pg_ready", 1, "b"))
                pe.wait_ge(read["T"], r.claim("T", "b_pgt"))
                for t in range(TILES):
                    last = nc.tensor.transpose(T[:, t * P:(t + 1) * P], pg[:, t * H:(t + 1) * H, :].rearrange("p h g -> p (h g)"), ident)
                last.then_inc(full["T"], 1)

            def global_values(r):
                pe.wait_ge(sems["xgr_ready"], r.nth("xgr_ready", 1, "b"))
                pe.wait_ge(read["T"], r.claim("T", "b_vg"))
                nc.tensor.matmul(T[:, 0:P], xgr[:, :, :].rearrange("p h g -> p (h g)"), wv_s[:, :], start=True, stop=True,
                                 skip_group_check=True).then_inc(full["T"], 1)

            def logits(r, stage, n):
                use = f"{stage}_s{n}"
                s, pb = s_bank[use], r.buf(stage)
                if n == 0 and stage == "b":
                    pe.wait_ge(sems["k_stacked"], r.nth("k_stacked", 16, "b"))
                    pe.wait_ge(sems["q_spread"], r.nth("q_spread", 4 * 16, "b"))
                if n == 0 and stage == "c":
                    pe.wait_ge(sems["max_placed"], r.nth("max_placed", 4 * 16, "c"))
                rows = STACK if stage == "b" else P
                pe.wait_ge(read[s], r.claim(s, use))
                mask = masksb[:, 1 if n == 0 else 2 if n == BLOCKS - 1 else 0, :].unsqueeze(1).broadcast_to([P, 8, W])
                for half in range(2):
                    dst = bank[s][:, half * 512:(half + 1) * 512]
                    nc.tensor.matmul(dst, identb[:, :], mask, start=True, stop=False, skip_group_check=True)
                    for c in (2 * half, 2 * half + 1):
                        last = nc.tensor.matmul(dst[:, (c % 2) * 256:(c % 2 + 1) * 256], ks[pb][0:rows, c, n * W:n * W + P],
                                                qx[pb][0:rows, c, :, n * W:(n + 1) * W], start=False, stop=True, skip_group_check=True)
                last.then_inc(full[s], 1)

            def maxima_turned(r, half):
                s = f"b_s{4 * half + 3}"
                pe.wait_ge(read[s_bank[s]], r.emptied(s_bank[s], s))
                pe.wait_ge(read["O"], r.claim("O", f"b_mt{half}"))
                nc.tensor.transpose(O[:, 0:P], rmax[:, half, :, :, :].rearrange("p h n v -> p (h n v)"), ident).then_inc(sems["max_turned"], 1)

            def weigh(r, n):
                pb = r.buf("c")
                pe.wait_ge(read[s_bank[f"c_s{n}"]], r.emptied(s_bank[f"c_s{n}"], f"c_s{n}"))
                if n % 2 == 0:
                    pe.wait_ge(read["O"], r.claim("O", f"c_o{n // 2}"))
                for h in range(H):
                    j, c = h // 4, h % 4
                    last = nc.tensor.matmul(O[32 * c:32 * c + VW, j * P + (n % 2) * W:j * P + (n % 2 + 1) * W], va[pb][:, n, h, :],
                                            pr[n % 2][:, h, :], start=True, stop=True, skip_group_check=True)
                last.then_inc(sems["weighed"], 1)

            def weighed_turned(r, t):
                pe.wait_ge(read["O"], r.emptied("O", f"c_o{t}"))
                pe.wait_ge(read["T"], r.claim("T", f"c_ot{t}"))
                for j in range(4):
                    last = nc.tensor.transpose(T[:, j * P:(j + 1) * P], osb[t % 2][:, j * P:(j + 1) * P], ident)
                last.then_inc(full["T"], 1)

            def global_out(r, t):
                pe.wait_ge(read["Y0"], r.claim("Y0", f"c_og{t}"))
                pb = r.buf("c")
                nc.tensor.matmul(Y0[:, 0:P], pgt[pb][:, t * P:(t + 1) * P], vge[pb][:, :, :].rearrange("p h d -> p (h d)"), start=True,
                                 stop=True, skip_group_check=True).then_inc(full["Y0"], 1)

            def out_turned(r, t):
                pe.wait_ge(read["Y0"], r.emptied("Y0", f"c_og{t}"))
                pe.wait_ge(read["Y1"], r.claim("Y1", f"c_bt{t}"))
                nc.tensor.transpose(Y1[:, 0:P], og[t % 2][:, :], ident).then_inc(full["Y1"], 1)

            def project(r, t):
                pe.wait_ge(read["Y1"], r.emptied("Y1", f"c_bt{t}"))
                pe.wait_ge(read["Y0"], r.claim("Y0", f"c_wo{t}"))
                nc.tensor.matmul(Y0[:, 0:P], bt[t % 2][:, :], wo_s[:, :], start=True, stop=True, skip_group_check=True)\
                    .then_inc(full["Y0"], 1)

            def body(r):
                p, a, b, c, d = (s in r.stages for s in "pabcd")
                if b:
                    turn(r, 1, "b_nt", "b")
                if c:
                    logits(r, "c", 0)
                if a:
                    turn(r, 0, "a_xt", "a")
                if c:
                    logits(r, "c", 1)
                if b:
                    q_k(r)
                if c:
                    weigh(r, 0)
                if a:
                    gate(r, 0, "a")
                if c:
                    logits(r, "c", 2)
                if b:
                    values(r)
                if c:
                    weigh(r, 1)
                if a:
                    locations(r, 0, "a")
                if c:
                    logits(r, "c", 3)
                if b:
                    global_logits(r)
                if c:
                    weigh(r, 2)
                if a:
                    gates_turned(r, 0, "a")
                if c:
                    logits(r, "c", 4)
                if a:
                    bias(r, 0, "a")
                if c:
                    weigh(r, 3)
                    weighed_turned(r, 0)
                    global_out(r, 0)
                    logits(r, "c", 5)
                    out_turned(r, 0)
                if b:
                    global_turned(r)
                if c:
                    weigh(r, 4)
                    project(r, 0)
                    logits(r, "c", 6)
                if b:
                    global_values(r)
                if a:
                    experts(r, 0, "a", 0)
                if c:
                    weigh(r, 5)
                    weighed_turned(r, 1)
                    global_out(r, 1)
                    logits(r, "c", 7)
                    out_turned(r, 1)
                    weigh(r, 6)
                    project(r, 1)
                if b:
                    logits(r, "b", 0)
                if a:
                    experts(r, 0, "a", 1)
                if c:
                    weigh(r, 7)
                    weighed_turned(r, 2)
                    global_out(r, 2)
                if b:
                    logits(r, "b", 1)
                if c:
                    out_turned(r, 2)
                if b:
                    logits(r, "b", 2)
                if c:
                    project(r, 2)
                    weighed_turned(r, 3)
                    global_out(r, 3)
                if b:
                    logits(r, "b", 3)
                if c:
                    out_turned(r, 3)
                    project(r, 3)
                if a:
                    experts(r, 0, "a", 2)
                if b:
                    logits(r, "b", 4)
                if a:
                    experts(r, 0, "a", 3)
                if b:
                    logits(r, "b", 5)
                if d:
                    turn(r, 2, "d_xt", "d")
                if b:
                    maxima_turned(r, 0)
                if d:
                    gate(r, 1, "d")
                if b:
                    logits(r, "b", 6)
                if d:
                    experts(r, 1, "d", 0)
                if b:
                    logits(r, "b", 7)
                if d:
                    locations(r, 1, "d")
                    gates_turned(r, 1, "d")
                    bias(r, 1, "d")
                if b:
                    maxima_turned(r, 1)
                if d:
                    experts(r, 1, "d", 1)
                    experts(r, 1, "d", 2)
                    experts(r, 1, "d", 3)

            rounds(pe, body)

        @block.scalar
        def _(act):
            act.wait_ge(consts_ready, NCONSTS_READY)

            def evacuate(r, n, use, dst, src, scale=1.0):
                act.wait_ge(full[n], r.filled(n, use))
                nc.scalar.activation(dst, src, ACT.Copy, scale=scale).then_inc(read[n], 1)

            def normalise(r, f, stage, src):
                act.wait_ge(sems[f"shift_ready{f}"], r.nth(f"shift_ready{f}", 1, stage))
                for t in range(TILES):
                    nc.scalar.activation(xn[f][:, t, :], src[:, t, :], ACT.Identity, bias=shift[f][:, t:t + 1], scale=rstd[f][:, t:t + 1])\
                        .then_inc(sems[f"xn_ready{f}"], 1)

            def exp(r, n):
                use = f"c_s{n}"
                s = s_bank[use]
                act.wait_ge(full[s], r.filled(s, use))
                if n >= 2:
                    act.wait_ge(sems["weighed"], r.nth("weighed", n - 1, "c"))
                else:
                    if r.ran("c"):
                        act.wait_ge(sems["weighed"], r.last("weighed", "c"))
                nc.scalar.activation(pr[n % 2][:, :, :].rearrange("p h w -> p (h w)"), bank[s][:, :], ACT.Exp).then_inc(read[s], 1)

            def gate_exp(r, f, stage):
                act.wait_ge(read["T"], r.emptied("T", f"{stage}_gate"))
                nc.scalar.activation(lexp[f][:, :, :], lsub[f][:, :, :], ACT.Exp).then_inc(sems[f"lexp_ready{f}"], 1)

            def fp32_qk(r):
                evacuate(r, "Y0", "b_q", qf[:, :], Y0[:, :], scale=SCALE)
                evacuate(r, "Y1", "b_k", kf[:, :], Y1[:, :])

            def higher_parts(r):
                if r.ran("b"):
                    act.wait_ge(sems["q_in_dram"], r.last("q_in_dram", "b"))
                if r.ran("b"):
                    act.wait_ge(sems["k_in_dram"], r.last("k_in_dram", "b"))
                act.wait_ge(read["Y0"], r.emptied("Y0", "b_q"))
                nc.scalar.activation(q3[:, 0:3:2, :], qf[:, :].unsqueeze(1).broadcast_to([P, 2, SEQ]), ACT.Copy).then_inc(sems["q_hi_ready"], 1)
                act.wait_ge(read["Y1"], r.emptied("Y1", "b_k"))
                nc.scalar.activation(k3[:, 0:2, HALO:HALO + SEQ], kf[:, :].unsqueeze(1).broadcast_to([P, 2, SEQ]), ACT.Copy)\
                    .then_inc(sems["k_hi_ready"], 1)

            def global_tokens(r):
                act.wait_ge(read["T"], r.emptied("T", "b_nt"))
                nc.scalar.activation(xgr[:, :, :], nt[:, HALO:HALO + SEQ:W].unsqueeze(1).broadcast_to([P, H, G]), ACT.Copy)\
                    .then_inc(sems["xgr_ready"], 1)

            def values(r):
                for n in range(2):
                    evacuate(r, f"Y{n}", f"b_v{n}", va[r.buf("b")][:, 4 * n:4 * n + 4, :, 0:DH],
                             bank[f"Y{n}"][:, :].rearrange("p (n h d) -> p n h d", n=4, h=H))

            def global_exp(r):
                act.wait_ge(read["T"], r.emptied("T", "b_lg"))
                nc.scalar.activation(lge[:, :, :], lgs[:, :, :], ACT.Exp).then_inc(sems["lge_ready"], 1)

            def pair(r, t):
                act.wait_ge(sems["weighed"], r.nth("weighed", 2 * t + 2, "c"))
                nc.scalar.activation(osb[t % 2][:, :], O[:, :], ACT.Copy).then_inc(read["O"], 1)

            def body(r):
                p, a, b, c, d = (s in r.stages for s in "pabcd")
                if b:
                    evacuate(r, "T", "b_nt", nt[:, HALO:HALO + SEQ], T[:, :])
                if c:
                    exp(r, 0)
                if a:
                    evacuate(r, "T", "a_xt", xt[0][:, :], T[:, :])
                if b:
                    fp32_qk(r)
                if c:
                    exp(r, 1)
                if b:
                    higher_parts(r)
                if c:
                    exp(r, 2)
                if a:
                    gate_exp(r, 0, "a")
                if b:
                    values(r)
                    global_tokens(r)
                if c:
                    exp(r, 3)
                    pair(r, 0)
                if b:
                    global_exp(r)
                if c:
                    exp(r, 4)
                if a:
                    evacuate(r, "T", "a_gmt", gmt[0][:, :], T[0:TILES * E, 0:P])
                if c:
                    pair(r, 1)
                    exp(r, 5)
                    evacuate(r, "Y1", "c_bt0", bt[0][:, :], Y1[:, 0:P])
                if b:
                    evacuate(r, "T", "b_pgt", pgt[r.buf("b")][:, :], T[:, :])
                if c:
                    exp(r, 6)
                    pair(r, 2)
                    exp(r, 7)
                    evacuate(r, "Y1", "c_bt1", bt[1][:, :], Y1[:, 0:P])
                if p:
                    normalise(r, 0, "p", x0[r.buf("p")])
                if c:
                    pair(r, 3)
                    evacuate(r, "Y1", "c_bt2", bt[0][:, :], Y1[:, 0:P])
                    evacuate(r, "Y1", "c_bt3", bt[1][:, :], Y1[:, 0:P])
                if d:
                    normalise(r, 2, "d", x2)
                    evacuate(r, "T", "d_xt", xt[1][:, :], T[:, :])
                    gate_exp(r, 1, "d")
                if a:
                    normalise(r, 1, "a", x1[r.buf("a")])
                if d:
                    evacuate(r, "T", "d_gmt", gmt[1][:, :], T[0:TILES * E, 0:P])

            rounds(act, body)

        @block.vector
        def _(dve):
            nc.vector.memset(bexp_s[:, :], 0.0).then_inc(zeros_ready, 1)
            for i in range(2):
                nc.vector.memset(qx[i][:, :, :, :], 0.0).then_inc(consts_ready, 1)
                nc.vector.memset(ks[i][0:STACK, :, :], 0.0).then_inc(consts_ready, 1)
                nc.vector.memset(ks[i][STACK:P, :, :], 1.0).then_inc(consts_ready, 1)
            nc.vector.memset(k3[:, :, :], 0.0).then_inc(consts_ready, 1)
            nc.vector.memset(nt[:, :], 0.0).then_inc(consts_ready, 1)
            for f in range(2):
                nc.vector.memset(carry[f][:, :], 0.0).then_inc(consts_ready, 1)
            for n in bank:
                nc.vector.memset(bank[n][:, :], 0.0).then_inc(read[n], 1)
            dve.wait_ge(consts_loaded, 12 * 16)
            nc.vector.tensor_copy(identb[:, :], cst[:, IDENT:IDENT + P]).then_inc(consts_ready, 1)
            nc.vector.tensor_copy(trib[:, :], cst[:, TRI:TRI + P]).then_inc(consts_ready, 1)
            nc.vector.tensor_copy(onesb[:, :], cst[:, ONES:ONES + P]).then_inc(consts_ready, 1)
            nc.vector.tensor_copy(masksb[:, :, :].rearrange("p m w -> p (m w)"), cst[:, MASKS:MASKS + 3 * W]).then_inc(consts_ready, 1)
            dve.wait_ge(consts_ready, NCONSTS_READY)

            def statistics(r, f, stage, src):
                for t in range(TILES):
                    last = nc.vector.bn_stats(st[f][:, t, :], src[:, t, :])
                last.then_inc(steps[stage], 1)
                dve.wait_ge(steps[stage], r.step(stage, r.mark(stage)))
                dve.nop(nofuse=True)
                for t in range(TILES):
                    last = nc.vector.bn_aggr(mv[f][:, t, :], st[f][:, t, :])
                last.then_inc(steps[stage], 1)
                dve.wait_ge(steps[stage], r.step(stage, r.mark(stage)))
                nc.vector.tensor_scalar(ve[f][:, :], mv[f][:, :, 1], EPS, None, ALU.add).then_inc(sems[f"var_ready{f}"], 1)

            def shifts(r, f, stage):
                dve.wait_ge(sems[f"rstd_ready{f}"], r.nth(f"rstd_ready{f}", 1, stage))
                nc.vector.scalar_tensor_tensor(out=shift[f][:, :], in0=mv[f][:, :, 0], scalar=-1.0, in1=rstd[f][:, :], op0=ALU.mult,
                                               op1=ALU.mult).then_inc(sems[f"shift_ready{f}"], 1)

            def each(ap):
                return ap.unsqueeze(2).broadcast_to([P, TILES, E])

            def route(r, f, stage):
                g = T[:, 0:TILES * E].rearrange("p (t e) -> p t e", e=E)
                dve.wait_ge(full["T"], r.filled("T", f"{stage}_gate"))
                nc.vector.tensor_reduce(lmax[f][:, :], g, AX.X, ALU.max).then_inc(steps[stage], 1)
                dve.wait_ge(steps[stage], r.step(stage, r.mark(stage)))
                nc.vector.tensor_tensor(lsub[f][:, :, :], g, each(lmax[f][:, :]), ALU.subtract).then_inc(read["T"], 1)

            def choose(r, f, stage):
                dve.wait_ge(sems[f"lexp_ready{f}"], r.nth(f"lexp_ready{f}", 1, stage))
                nc.vector.tensor_reduce(lsum[f][:, :], lexp[f][:, :, :], AX.X, ALU.add).then_inc(steps[stage], 1)
                a = r.mark(stage)
                nc.vector.scalar_tensor_tensor(out=top[f][:, :, :], in0=lexp[f][:, :, :], scalar=1.0,
                                               in1=first.unsqueeze(1).broadcast_to([P, TILES, E]), op0=ALU.is_ge, op1=ALU.mult).then_inc(steps[stage], 1)
                b = r.mark(stage)
                dve.wait_ge(steps[stage], r.step(stage, a))
                nc.vector.reciprocal(prob[f][:, :], lsum[f][:, :])
                dve.wait_ge(steps[stage], r.step(stage, b))
                nc.vector.tensor_reduce(topm[f][:, :], top[f][:, :, :], AX.X, ALU.max).then_inc(steps[stage], 1)
                dve.wait_ge(steps[stage], r.step(stage, r.mark(stage)))
                nc.vector.tensor_tensor(hot[f][:, :, :], top[f][:, :, :], each(topm[f][:, :]), ALU.is_equal).then_inc(steps[stage], 1)
                dve.wait_ge(steps[stage], r.step(stage, r.mark(stage)))
                nc.vector.tensor_copy(hotb[f][:, :, :], hot[f][:, :, :]).then_inc(sems[f"hot_ready{f}"], 1)

            def keep(r, f, stage):
                n = TILES * E
                dve.wait_ge(full["T"], r.filled("T", f"{stage}_loc"))
                nc.vector.tensor_tensor(loc[f][:, :, :], T[:, 0:n].rearrange("p (t e) -> p t e", e=E),
                                        carry[f][:, :].unsqueeze(1).broadcast_to([P, TILES, E]), ALU.add).then_inc(steps[stage], 1)
                a = r.mark(stage)
                dve.wait_ge(steps[stage], r.step(stage, a))
                nc.vector.tensor_tensor(carry[f][:, :], carry[f][:, :], T[:, n:n + E], ALU.add).then_inc(read["T"], 1)
                nc.vector.scalar_tensor_tensor(out=top[f][:, :, :], in0=loc[f][:, :, :], scalar=float(CAP), in1=hot[f][:, :, :],
                                               op0=ALU.is_lt, op1=ALU.mult).then_inc(steps[stage], 1)
                dve.wait_ge(steps[stage], r.step(stage, r.mark(stage)))
                nc.vector.scalar_tensor_tensor(out=gm[f][:, :, :], in0=top[f][:, :, :], scalar=0.5, in1=each(prob[f][:, :]),
                                               op0=ALU.mult, op1=ALU.mult).then_inc(sems[f"gm_ready{f}"], 1)

            def residual(r, f, stage, src):
                dve.wait_ge(full["T"], r.filled("T", f"{stage}_bias"))
                nc.vector.tensor_tensor(acc[f][:, :, :], T[:, :].rearrange("p (t c) -> p t c", t=TILES), src[:, :, :], ALU.add)\
                    .then_inc(read["T"], 1)

            def combine(r, f, stage, t, dst, done):
                dve.wait_ge(read["T"], r.emptied("T", f"{stage}_bias"))
                marks = {}
                for e in range(E):
                    n = f"Y{e // 4}"
                    if e % 4 == 0:
                        dve.wait_ge(full[n], r.filled(n, f"{stage}_exp{t}"))
                    src = bank[n][:, (e % 4) * P:(e % 4 + 1) * P]
                    if e == 5:
                        dve.wait_ge(read["Y0"], r.emptied("Y0", f"{stage}_exp{t}"))
                    elif e >= 2:
                        dve.wait_ge(steps[stage], r.step(stage, marks[e - 2]))
                    if e == 1:
                        ins = nc.vector.tensor_scalar(odd[f][:, t, :], src, gm[f][:, t, e:e + 1], None, ALU.mult)
                    else:
                        s = (odd if e % 2 else acc)[f]
                        ins = nc.vector.scalar_tensor_tensor(out=s[:, t, :], in0=src, scalar=gm[f][:, t, e:e + 1], in1=s[:, t, :],
                                                             op0=ALU.mult, op1=ALU.add)
                    if e % 4 == 3:
                        ins.then_inc(read[n], 1)
                    else:
                        ins.then_inc(steps[stage], 1)
                        marks[e] = r.mark(stage)
                dve.wait_ge(steps[stage], r.step(stage, marks[6]))
                dve.wait_ge(read["Y1"], r.emptied("Y1", f"{stage}_exp{t}"))
                nc.vector.tensor_tensor(dst[:, t, :], acc[f][:, t, :], odd[f][:, t, :], ALU.add).then_inc(sems[done], 1)

            def lower_parts(r):
                dve.wait_ge(sems["q_hi_ready"], r.nth("q_hi_ready", 1, "b"))
                nc.vector.tensor_tensor(q3[:, 1, :], qf[:, :], q3[:, 0, :], ALU.subtract).then_inc(sems["q_lo_ready"], 1)
                dve.wait_ge(sems["k_hi_ready"], r.nth("k_hi_ready", 1, "b"))
                nc.vector.tensor_tensor(k3[:, 2, HALO:HALO + SEQ], kf[:, :], k3[:, 0, HALO:HALO + SEQ], ALU.subtract)\
                    .then_inc(sems["k_lo_ready"], 1)
                nc.vector.tensor_tensor(kge[:, :, :], heads.unsqueeze(2).broadcast_to([P, H, G]),
                                        kf[:, ::W].unsqueeze(1).broadcast_to([P, H, G]), ALU.mult).then_inc(sems["kge_ready"], 1)

            def all_g(ap):
                return ap.unsqueeze(2).broadcast_to([P, TILES * H, G])

            def global_shift(r):
                lg = T[:, :].rearrange("p (th g) -> p th g", g=G)
                dve.wait_ge(full["T"], r.filled("T", "b_lg"))
                nc.vector.tensor_reduce(lgm[:, :], lg, AX.X, ALU.max).then_inc(steps["b"], 1)
                dve.wait_ge(steps["b"], r.step("b", r.mark("b")))
                nc.vector.tensor_tensor(lgs[:, :, :], lg, all_g(lgm[:, :]), ALU.subtract).then_inc(read["T"], 1)

            def global_probs(r):
                dve.wait_ge(sems["lge_ready"], r.nth("lge_ready", 1, "b"))
                nc.vector.tensor_reduce(lgr[:, :], lge[:, :, :], AX.X, ALU.add).then_inc(steps["b"], 1)
                dve.wait_ge(steps["b"], r.step("b", r.mark("b")))
                nc.vector.reciprocal(lgi[:, :], lgr[:, :]).then_inc(steps["b"], 1)
                dve.wait_ge(steps["b"], r.step("b", r.mark("b")))
                nc.vector.tensor_tensor(pg[:, :, :], lge[:, :, :], all_g(lgi[:, :]), ALU.mult).then_inc(sems["pg_ready"], 1)

            def global_values(r):
                dve.wait_ge(full["T"], r.filled("T", "b_vg"))
                nc.vector.tensor_tensor(vge[r.buf("b")][:, :, :], T[:, 0:P].rearrange("p (h d) -> p h d", d=DH),
                                        heads.unsqueeze(2).broadcast_to([P, H, DH]), ALU.mult).then_inc(read["T"], 1)

            def block_max(r, n):
                use = f"b_s{n}"
                s = s_bank[use]
                dve.wait_ge(full[s], r.filled(s, use))
                nc.vector.tensor_reduce(rmax[:, n // 4, :, n % 4, :], bank[s][:, :].rearrange("p (h v q) -> p h v q", v=2, q=32), AX.X,
                                        ALU.max, apply_transpose=True).then_inc(read[s], 1)

            def query_max(r, half):
                dve.wait_ge(sems["max_turned"], r.nth("max_turned", half + 1, "b"))
                nc.vector.tensor_reduce(nmax[:, half, :], O[:, 0:P].rearrange("p (k q) -> p q k", k=4), AX.X, ALU.max, negate=True)\
                    .then_inc(read["O"], 1)

            def normalise(r, t):
                dve.wait_ge(full["T"], r.filled("T", f"c_ot{t}"))
                o = T[:, :].rearrange("p (h u) -> p h u", u=32)
                nc.vector.reciprocal(rl[t % 2][:, :], o[:, :, DH]).then_inc(steps["c"], 1)
                dve.wait_ge(steps["c"], r.step("c", r.mark("c")))
                nc.vector.tensor_tensor(ol[t % 2][:, :, :], o[:, :, 0:DH], rl[t % 2][:, :].unsqueeze(2).broadcast_to([P, H, DH]), ALU.mult)\
                    .then_inc(read["T"], 1)
                dve.wait_ge(full["Y0"], r.filled("Y0", f"c_og{t}"))
                dve.wait_ge(read["T"], r.emptied("T", f"c_ot{t}"))
                nc.vector.tensor_tensor(og[t % 2][:, :], ol[t % 2][:, :, :].rearrange("p h d -> p (h d)"), Y0[:, 0:P], ALU.add)\
                    .then_inc(read["Y0"], 1)

            def attention_out(r, t):
                dve.wait_ge(full["Y0"], r.filled("Y0", f"c_wo{t}"))
                nc.vector.tensor_tensor(x2[:, t, :], Y0[:, 0:P], x1b[r.buf("c")][:, t, :], ALU.add).then_inc(read["Y0"], 1)

            def layernorm_x(r):
                dve.wait_ge(sems["x_loaded"], r.nth("x_loaded", 16, "p"))
                statistics(r, 0, "p", x0[r.buf("p")])

            def layernorm_x1(r):
                dve.wait_ge(sems["x1_ready"], r.nth("x1_ready", TILES, "a"))
                statistics(r, 1, "a", x1[r.buf("a")])

            def layernorm_x2(r):
                dve.wait_ge(read["Y0"], r.emptied("Y0", "c_wo3"))
                statistics(r, 2, "d", x2)

            def combine_out(r):
                if r.ran("d"):
                    dve.wait_ge(sems["stored"], r.last("stored", "d"))
                for t in range(TILES):
                    combine(r, 1, "d", t, y, "y_ready")

            def body(r):
                p, a, b, c, d = (s in r.stages for s in "pabcd")
                if b:
                    lower_parts(r)
                if a:
                    route(r, 0, "a")
                    choose(r, 0, "a")
                    keep(r, 0, "a")
                if b:
                    global_shift(r)
                    global_probs(r)
                if a:
                    residual(r, 0, "a", x0[r.buf("a")])
                if c:
                    normalise(r, 0)
                    attention_out(r, 0)
                if b:
                    global_values(r)
                if a:
                    combine(r, 0, "a", 0, x1[r.buf("a")], "x1_ready")
                if c:
                    normalise(r, 1)
                if p:
                    layernorm_x(r)
                if c:
                    attention_out(r, 1)
                if a:
                    combine(r, 0, "a", 1, x1[r.buf("a")], "x1_ready")
                if b:
                    block_max(r, 0)
                if p:
                    shifts(r, 0, "p")
                if c:
                    normalise(r, 2)
                if b:
                    block_max(r, 1)
                if c:
                    attention_out(r, 2)
                if b:
                    block_max(r, 2)
                if c:
                    normalise(r, 3)
                if b:
                    block_max(r, 3)
                if c:
                    attention_out(r, 3)
                if d:
                    layernorm_x2(r)
                if a:
                    combine(r, 0, "a", 2, x1[r.buf("a")], "x1_ready")
                if d:
                    shifts(r, 2, "d")
                if b:
                    block_max(r, 4)
                if a:
                    combine(r, 0, "a", 3, x1[r.buf("a")], "x1_ready")
                    layernorm_x1(r)
                if b:
                    block_max(r, 5)
                if a:
                    shifts(r, 1, "a")
                if d:
                    route(r, 1, "d")
                if b:
                    block_max(r, 6)
                    query_max(r, 0)
                if d:
                    choose(r, 1, "d")
                if b:
                    block_max(r, 7)
                if d:
                    keep(r, 1, "d")
                    residual(r, 1, "d", x2)
                if b:
                    query_max(r, 1)
                if d:
                    combine_out(r)
                for s, n in DVE_STEPS.items():
                    assert s not in r.stages or r.steps[s] == n, (s, r.steps[s])

            rounds(dve, body)


DVE_STEPS = {"p": 2, "a": 33, "b": 3, "c": 4, "d": 33}
NCONSTS_READY = 3 + 14


def constants(np):
    c = np.zeros((P, NCONST), np.float32)
    k = np.arange(P)[:, None]
    c[:, IDENT:IDENT + P] = np.eye(P)
    c[:, TRI:TRI + P] = k < np.arange(P)[None]
    c[:, ONES:ONES + P] = 1.0
    band = (k >= np.arange(W)[None]) & (k - np.arange(W)[None] <= W - 1)
    inside = [k >= 0, k >= HALO, k < P - HALO]
    for m in range(3):
        c[:, MASKS + m * W:MASKS + (m + 1) * W] = np.where(band & inside[m], 0.0, NEG)
    c[:, HEADS:HEADS + H] = k // DH == np.arange(H)[None]
    c[:, FIRST:FIRST + E] = E - np.arange(E)
    return c


def kernel(**inputs):
    import numpy as np
    import concourse.bacc as bacc
    from concourse.bass_utils import run_bass_kernel_spmd

    a = {k: np.asarray(v) for k, v in inputs.items()}
    w_qkv = a["L0_attn_w_qkv"]
    arrays = {
        "x": a["L0_attn_x"],
        "w_q": w_qkv[:, 0:P], "w_k": w_qkv[:, P:2 * P], "w_v": w_qkv[:, 2 * P:3 * P],
        "w_out": a["L0_attn_w_out"],
        "b_out": np.broadcast_to(a["L0_attn_b_out"], (P, P)),
        "w_gate": a["L0_ffn_wg"],
        "w_exp": a["L0_ffn_W"].transpose(2, 0, 1).reshape(P, E * P),
        "b_exp": a["L0_ffn_b"],
        "const": constants(np),
    }
    nc = bacc.Bacc("TRN2", target_bir_lowering=False, num_devices=1)
    arrays = {f"in_{n}": np.ascontiguousarray(v) for n, v in arrays.items()}
    aps = [nc.dram_tensor(n, v.shape, mybir.dt.from_np(v.dtype), kind="ExternalInput").ap() for n, v in arrays.items()]
    out = nc.dram_tensor("out", (NB, SEQ, P), F32, kind="ExternalOutput").ap()
    build(nc, *aps, out)
    r = run_bass_kernel_spmd(nc, [arrays], core_ids=[0])
    return r.results[0]["out"]
```

```python
from contextlib import ExitStack

import concourse.bass as bass
from concourse import mybir

F32 = mybir.dt.float32
F16 = mybir.dt.float16
BF16 = mybir.dt.bfloat16
ALU = mybir.AluOpType
ACT = mybir.ActivationFunctionType
AX = mybir.AxisListType

P = 128
NB = 8
SEQ = 512
TILES = SEQ // P
E = 8
CAP = NB * SEQ // E
H = 16
DH = P // H
W = 64
BLOCKS = SEQ // W
HALO = W // 2
KEYS = SEQ + 2 * HALO
G = SEQ // W
C4 = H // 4
ROUTES = TILES * 2 * E
TERMS = 3
STACK = 4 * DH * TERMS
SCALE = float(DH) ** -0.5
EPS = 1e-5
NEG = -1.0e9
WSCALE = 16.0
VW = DH + 1

IDENT = 0
TRI = IDENT + P
ONES = TRI + P
MASKS = ONES + P
HEADS = MASKS + 3 * W
FIRST = HEADS + H
NCONST = FIRST + E

USES = {
    "T": "e_xt b_nt a_xt g_gate b_lg g_loc g_gmt a_bias e_bias c_ot0 c_ot1 c_ot2 c_ot3 b_pgt b_vg".split(),
    "Y0": "b_q b_v0 c_og0 a_exp0 c_wo0 c_og1 a_exp1 c_wo1 e_exp0 c_og2 a_exp2 c_wo2 e_exp1 c_og3 a_exp3 c_wo3 e_exp2 e_exp3".split(),
    "Y1": "b_k b_v1 c_bt0 a_exp0 c_bt1 a_exp1 e_exp0 c_bt2 a_exp2 e_exp1 c_bt3 a_exp3 e_exp2 e_exp3".split(),
    "O": "c_o0 c_o1 c_o2 c_o3 b_mt0 b_mt1".split(),
    "S0": "c_s0 c_s2 c_s4 c_s6 b_s0 b_s2 b_s4 b_s6".split(),
    "S1": "c_s1 c_s3 c_s5 c_s7 b_s1 b_s3 b_s5 b_s7".split(),
}


def build(nc, x, w_q, w_k, w_v, w_out, b_out, w_gate, w_exp, b_exp, const, out):
    x_v = x.rearrange("b (t p) c -> b p t c", p=P)
    out_v = out.rearrange("b (t p) c -> b p t c", p=P)

    with ExitStack() as ctx:
        def sb(name, shape, dt=F32):
            return ctx.enter_context(nc.sbuf_tensor(name, shape, dt))

        def sem(name):
            return ctx.enter_context(nc.semaphore(name))

        q_dram = nc.dram_tensor("q_parts", (P, TERMS, SEQ), F16).ap()
        k_dram = nc.dram_tensor("k_parts", (P, TERMS, KEYS), F16).ap()
        m_dram = nc.dram_tensor("max_parts", (H, 2, 8, 32), F16).ap()

        wq_s, wk_s, wv_s, wo_s = (sb(n, [P, P]) for n in ("wq_s", "wk_s", "wv_s", "wo_s"))
        bout_s = sb("bout_s", [P, P])
        wg_s = sb("wg_s", [P, E])
        we_s = sb("we_s", [P, E * P])
        we_hi, we_lo = (sb(n, [P, E * P], F16) for n in ("we_hi", "we_lo"))
        bexp_s = sb("bexp_s", [ROUTES, 2, TILES, P])
        cst = sb("cst", [P, NCONST])
        ident = cst[:, IDENT:IDENT + P]
        heads = cst[:, HEADS:HEADS + H]
        first = cst[:, FIRST:FIRST + E]
        identb = sb("identb", [P, P], BF16)
        trib = sb("trib", [P, P], BF16)
        onesb = sb("onesb", [P, P], BF16)
        masksb = sb("masksb", [P, 3, W], BF16)
        mhalf = sb("mhalf", [P, TILES])

        x0 = [sb(f"x0_{i}", [P, TILES, P]) for i in range(2)]
        x1 = [sb(f"x1_{i}", [P, TILES, P]) for i in range(2)]
        x2 = sb("x2", [P, TILES, P])
        y = sb("y", [P, TILES, P])
        st = [sb(f"st{f}", [P, TILES, 6]) for f in range(3)]
        mv = [sb(f"mv{f}", [P, TILES, 2]) for f in range(3)]
        ve = [sb(f"ve{f}", [P, TILES]) for f in range(3)]
        rstd = [sb(f"rstd{f}", [P, TILES]) for f in range(3)]
        xn = [sb(f"xn{f}", [P, TILES, P]) for f in range(3)]
        xt = [sb(f"xt{f}", [P, SEQ]) for f in range(2)]
        xt_hi = [sb(f"xt_hi{f}", [P, SEQ], F16) for f in range(2)]
        xt_lo = [sb(f"xt_lo{f}", [P, SEQ], F16) for f in range(2)]
        carry = sb("carry", [P, 2, E])
        lmax = sb("lmax", [P, TILES, 2])
        lsub = sb("lsub", [P, TILES, 2, E])
        lexp = sb("lexp", [P, TILES, 2, E])
        lsum = sb("lsum", [P, TILES, 2])
        prob = sb("prob", [P, TILES, 2])
        top = sb("top", [P, TILES, 2, E])
        topm = sb("topm", [P, TILES, 2])
        hot = sb("hot", [P, TILES, 2, E])
        hotb = sb("hotb", [P, TILES, 2, E], BF16)
        loc = sb("loc", [P, TILES, 2, E])
        gm_all = sb("gm_all", [P, P])
        gm = gm_all[:, 0:ROUTES].rearrange("p (t f e) -> p t f e", f=2, e=E)
        gmt = sb("gmt", [ROUTES, P])
        gms = sb("gms", [P, TILES, 2, E])
        acc = [sb(f"acc{f}", [P, TILES, P]) for f in range(2)]
        odd = [sb(f"odd{f}", [P, TILES, P]) for f in range(2)]
        scaled = [sb(f"scaled{f}", [P, 2, (1 + f) * E // 2, P]) for f in range(2)]
        fours = sb("fours", [P, 4, P])
        twos = [sb(f"twos{f}", [P, 2, P]) for f in range(2)]
        ones = [sb(f"ones{f}", [P, P]) for f in range(2)]

        nt = sb("nt", [P, KEYS])
        qf = sb("qf", [P, SEQ])
        kf = sb("kf", [P, SEQ])
        q3 = sb("q3", [P, TERMS, SEQ], F16)
        k3 = sb("k3", [P, TERMS, KEYS], F16)
        kge = sb("kge", [P, H, G])
        xgr = sb("xgr", [P, H, G])
        lgm = sb("lgm", [P, TILES * H])
        lgs = sb("lgs", [P, TILES * H, G])
        lge = sb("lge", [P, TILES * H, G])
        lgr = sb("lgr", [P, TILES * H])
        lgi = sb("lgi", [P, TILES * H])
        pg = sb("pg", [P, TILES * H, G])
        rmax = sb("rmax", [P, 2, H, 4, 2])
        nmax = sb("nmax", [P, 2, 32], F16)
        qx = [sb(f"qx{i}", [P, C4, 4, SEQ], F16) for i in range(2)]
        ks = [sb(f"ks{i}", [P, C4, KEYS], F16) for i in range(2)]
        va = [sb(f"va{i}", [P, BLOCKS, H, VW]) for i in range(2)]
        pgt = [sb(f"pgt{i}", [P, SEQ]) for i in range(2)]
        vge = [sb(f"vge{i}", [P, H, DH]) for i in range(2)]
        x1b = [sb(f"x1b{i}", [P, TILES, P]) for i in range(2)]
        pr = [sb(f"pr{i}", [P, H, W]) for i in range(2)]
        osb = [sb(f"osb{i}", [P, SEQ]) for i in range(2)]
        rl = [sb(f"rl{i}", [P, H]) for i in range(2)]
        ol = [sb(f"ol{i}", [P, H, DH]) for i in range(2)]
        og = [sb(f"og{i}", [P, P]) for i in range(2)]
        bt = [sb(f"bt{i}", [P, P]) for i in range(2)]

        bank = {n: ctx.enter_context(nc.psum_tensor(f"bank_{n}", [P, 512], F32)) for n in ("T", "Y0", "Y1", "O")}
        for n in ("S0", "S1"):
            bank[n] = ctx.enter_context(nc.psum_tensor(f"bank_{n}", [P, 1024], F32))
        T, Y0, Y1, O = bank["T"], bank["Y0"], bank["Y1"], bank["O"]
        full = {n: sem(f"bank_full_{n}") for n in bank if n != "O"}
        read = {n: sem(f"bank_read_{n}") for n in bank}
        s_bank = {u: n for n in ("S0", "S1") for u in USES[n]}

        per, sems = {}, {}

        def signal(name, count):
            per[name] = count
            sems[name] = sem(name)

        consts_loaded, experts_loaded, weights_loaded, consts_ready, zeros_ready = (
            sem(n) for n in ("consts_loaded", "experts_loaded", "weights_loaded", "consts_ready", "zeros_ready"))
        experts_hi_ready, experts_lo_ready = sem("experts_hi_ready"), sem("experts_lo_ready")
        buffers_ready = [sem(f"buffers_ready{i}") for i in range(2)]
        for f in range(2):
            signal(f"xt_hi_ready{f}", 1)
            signal(f"xt_lo_ready{f}", 1)
        signal("first_four_ready", TILES)
        signal("lexp_ready", 1)
        signal("hot_ready", 1)
        signal("gm_ready", 1)
        for f in range(3):
            signal(f"var_ready{f}", 1)
            signal(f"rstd_ready{f}", 1)
            signal(f"xn_ready{f}", TILES)
        signal("x_loaded", 16)
        signal("x1_ready", TILES)
        signal("x1b_ready", 1)
        signal("q_hi_ready", 1)
        signal("k_hi_ready", 1)
        signal("q_lo_ready", 1)
        signal("k_lo_ready", 1)
        signal("q_in_dram", 16)
        signal("k_in_dram", 16)
        signal("k_stacked", 16)
        signal("q_spread", 4 * 16)
        for half in range(2):
            signal(f"max_in_dram{half}", 16)
            signal(f"max_placed{half}", 4 * 16)
        signal("max_turned", 2)
        signal("kge_ready", 1)
        signal("xgr_ready", 1)
        signal("lge_ready", 1)
        signal("pg_ready", 1)
        signal("weighed", BLOCKS)
        signal("y_ready", TILES)
        signal("stored", 16)
        steps = {s: sem(f"dve_steps_{s}") for s in DVE_STEPS}
        pool_steps = {s: sem(f"pool_steps_{s}") for s in "ae"}

        LAG = {"p": -1, "g": 0, "a": 0, "b": 1, "c": 2, "d": 2, "e": 3}

        class Round:

            def __init__(self, stages, i, parity):
                if "a" in stages or "e" in stages:
                    stages += "g"
                self.stages, self.i, self.parity = stages, i, parity
                self.steps = dict.fromkeys(DVE_STEPS, 0)
                self.claims = dict.fromkeys(USES, 0)
                self.order = {n: [u for u in USES[n] if u[0] in stages] for n in USES}

            def seq(self, stage):
                return self.i - LAG[stage]

            def buf(self, stage):
                return (self.parity + LAG[stage]) % 2

            def position(self, n, use):
                return self.uses_before(n) + self.order[n].index(use)

            def uses_before(self, n):
                before = 0
                for s in "gabcde":
                    count = sum(u[0] == s for u in USES[n])
                    before = before + count * (self.seq(s) if s in self.stages else min(max(self.seq(s), 0), NB))
                return before

            def nth(self, name, k, stage):
                return self.seq(stage) * per[name] + k

            def ran(self, stage, back=1):
                return type(self.i) is not int or self.seq(stage) >= back

            def last(self, name, stage, back=1):
                return (self.seq(stage) - back + 1) * per[name]

            def filled(self, n, use):
                return self.position(n, use) + 1

            def emptied(self, n, use):
                return self.position(n, use) + 2

            def ffns(self):
                return slice(0 if "a" in self.stages else 1, 2 if "e" in self.stages else 1)

            def both(self):
                return "a" in self.stages and "e" in self.stages

            def claim(self, n, use):
                assert self.order[n][self.claims[n]] == use, (n, use, self.order[n][self.claims[n]])
                self.claims[n] += 1
                return self.position(n, use) + 1

            def step(self, stage, k):
                return self.seq(stage) * DVE_STEPS[stage] + k

            def mark(self, stage):
                self.steps[stage] += 1
                return self.steps[stage]

        def rounds(eng, body, first={}):
            for stages, i in (("p", -1), ("pa", 0), ("pab", 1), ("pabcd", 2)):
                if i in first:
                    first[i]()
                body(Round(stages, i, i % 2))
            with eng.Fori(0, (NB - 4) // 2) as k:
                body(Round("pabcde", 2 * k + 3, 1))
                body(Round("pabcde", 2 * k + 4, 0))
            for stages, i in (("abcde", NB - 1), ("bcde", NB), ("cde", NB + 1), ("e", NB + 2)):
                body(Round(stages, i, i % 2))

        block = ctx.enter_context(nc.Block())

        @block.sync
        def _(sp):
            sp.dma_start(cst[:, :], const).then_inc(consts_loaded, 16)

            def weights():
                for dst, src in ((we_s, w_exp), (wg_s, w_gate)):
                    sp.dma_start(dst[:, :], src).then_inc(experts_loaded, 16)
                sp.wait_ge(zeros_ready, 1)
                for t in range(TILES):
                    for f in range(2):
                        at = (2 * t + f) * E
                        sp.dma_start(bexp_s[at:at + E, f, t, :], b_exp).then_inc(weights_loaded, 16)
                for dst, src in ((wq_s, w_q), (wk_s, w_k), (wv_s, w_v), (wo_s, w_out), (bout_s, b_out)):
                    sp.dma_start(dst[:, :], src).then_inc(weights_loaded, 16)

            def sequence(view, i):
                return view[i] if type(i) is int else view[bass.ds(i, 1)].rearrange("b p t c -> p (b t) c")

            def load(r):
                if r.ran("p"):
                    sp.wait_ge(sems["var_ready0"], r.last("var_ready0", "p"))
                    sp.nop(nofuse=True)
                if r.ran("p", 2):
                    sp.wait_ge(sems["x1_ready"], r.last("x1_ready", "p", 2))
                    sp.nop(nofuse=True)
                sp.dma_start(x0[r.buf("p")][:, :, :], sequence(x_v, r.seq("p"))).then_inc(sems["x_loaded"], 16)

            def stack(r):
                pb = r.buf("b")
                sp.wait_ge(sems["q_lo_ready"], r.nth("q_lo_ready", 1, "b"))
                sp.nop(nofuse=True)
                sp.dma_start(q_dram, q3[:, :, :]).then_inc(sems["q_in_dram"], 16)
                sp.wait_ge(sems["k_lo_ready"], r.nth("k_lo_ready", 1, "b"))
                sp.nop(nofuse=True)
                sp.dma_start(k_dram, k3[:, :, :]).then_inc(sems["k_in_dram"], 16)
                sp.wait_ge(sems["q_in_dram"], r.nth("q_in_dram", 16, "b"))
                sp.nop(nofuse=True)
                for j in range(4):
                    sp.dma_start(qx[pb][24 * j:24 * j + 24, :, j, :], q_dram.rearrange("(c j d) t w -> j (d t) c w", c=C4, j=4)[j])\
                        .then_inc(sems["q_spread"], 16)
                sp.wait_ge(sems["k_in_dram"], r.nth("k_in_dram", 16, "b"))
                sp.nop(nofuse=True)
                sp.dma_start(ks[pb][0:STACK, :, :], k_dram.rearrange("(c jd) t w -> (jd t) c w", c=C4)).then_inc(sems["k_stacked"], 16)

            def place_max(r):
                for half in range(2):
                    sp.wait_ge(read["O"], r.emptied("O", f"b_mt{half}"))
                    sp.nop(nofuse=True)
                    sp.dma_start(m_dram[:, half, :, :], nmax[:, half, :]).then_inc(sems[f"max_in_dram{half}"], 16)
                    sp.wait_ge(sems[f"max_in_dram{half}"], r.nth(f"max_in_dram{half}", 16, "b"))
                    sp.nop(nofuse=True)
                    for j in range(4):
                        sp.dma_start(qx[r.buf("b")][STACK + j:STACK + j + 1, :, j, half * SEQ // 2:(half + 1) * SEQ // 2],
                                     m_dram.rearrange("(c j) a u q -> a j c (u q)", j=4)[half, j].unsqueeze(0))\
                            .then_inc(sems[f"max_placed{half}"], 16)

            def store(r):
                sp.wait_ge(sems["y_ready"], r.nth("y_ready", TILES, "e"))
                sp.nop(nofuse=True)
                sp.dma_start(sequence(out_v, r.seq("e")), y[:, :, :]).then_inc(sems["stored"], 16)

            def body(r):
                if "p" in r.stages:
                    load(r)
                if "b" in r.stages:
                    stack(r)
                    place_max(r)
                if "e" in r.stages:
                    store(r)
                if "b" in r.stages:
                    sp.wait_ge(sems["max_placed1"], r.nth("max_placed1", 4 * 16, "b"))
                    sp.nop(nofuse=True)

            def buffers(i):
                sp.wait_ge(buffers_ready[i], 4 + 2 * (i == 0))
                sp.nop(nofuse=True)

            rounds(sp, body, {0: weights, 1: lambda: buffers(0), 2: lambda: buffers(1)})
            sp.wait_ge(sems["stored"], 16 * NB)

        @block.gpsimd
        def _(pool):
            nc.gpsimd.memset(mhalf[:, :], -0.5).then_inc(consts_ready, 1)
            nc.gpsimd.memset(bexp_s[:, :, :, :], 0.0).then_inc(zeros_ready, 1)
            pool.wait_ge(consts_ready, NCONSTS_READY)

            def clear(i):
                if i == 0:
                    nc.gpsimd.memset(nt[:, :], 0.0).then_inc(buffers_ready[i], 1)
                    nc.gpsimd.memset(k3[:, :, :], 0.0).then_inc(buffers_ready[i], 1)
                nc.gpsimd.memset(va[i][:, :, :, :], 1.0).then_inc(buffers_ready[i], 1)
                nc.gpsimd.memset(ks[i][0:STACK, :, :], 0.0).then_inc(buffers_ready[i], 1)
                nc.gpsimd.memset(qx[i][:, :, :, :], 0.0).then_inc(buffers_ready[i], 1)
                pool.wait_ge(buffers_ready[i], 3 + 2 * (i == 0))
                nc.gpsimd.memset(ks[i][STACK:P, :, :], 1.0).then_inc(buffers_ready[i], 1)
                pool.wait_ge(buffers_ready[i], 4 + 2 * (i == 0))

            def rsqrt(r, f, stage):
                pool.wait_ge(sems[f"var_ready{f}"], r.nth(f"var_ready{f}", 1, stage))
                nc.gpsimd.tensor_tensor(rstd[f][:, :], ve[f][:, :], mhalf[:, :], ALU.pow).then_inc(sems[f"rstd_ready{f}"], 1)

            def add_bias(r):
                pb = r.buf("b")
                pool.wait_ge(sems["x1_ready"], r.nth("x1_ready", TILES, "b"))
                nc.gpsimd.tensor_tensor(x1b[pb][:, :, :], x1[pb][:, :, :], bout_s[:, :].unsqueeze(1).broadcast_to([P, TILES, P]), ALU.add)\
                    .then_inc(sems["x1b_ready"], 1)

            def combine(r, t):
                pool.wait_ge(read["Y1"], r.emptied("Y1", f"a_exp{t}"))
                nc.gpsimd.tensor_tensor(twos[0][:, :, :], scaled[0][:, t % 2, 0:2, :], scaled[0][:, t % 2, 2:4, :], ALU.add)\
                    .then_inc(pool_steps["a"], 1)
                pool.wait_ge(pool_steps["a"], r.seq("a") * 2 * TILES + 2 * t + 1)
                nc.gpsimd.tensor_tensor(ones[0][:, :], twos[0][:, 0, :], twos[0][:, 1, :], ALU.add).then_inc(pool_steps["a"], 1)
                pool.wait_ge(pool_steps["a"], r.seq("a") * 2 * TILES + 2 * t + 2)
                pool.wait_ge(sems["first_four_ready"], r.nth("first_four_ready", t + 1, "a"))
                nc.gpsimd.tensor_tensor(x1[r.buf("a")][:, t, :], ones[0][:, :], acc[0][:, t, :], ALU.add).then_inc(sems["x1_ready"], 1)

            def combine_all(r, t):
                pool.wait_ge(read["Y1"], r.emptied("Y1", f"e_exp{t}"))
                nc.gpsimd.tensor_tensor(fours[:, :, :], scaled[1][:, t % 2, 0:4, :], scaled[1][:, t % 2, 4:8, :], ALU.add)\
                    .then_inc(pool_steps["e"], 1)
                pool.wait_ge(pool_steps["e"], r.seq("e") * 3 * TILES + 3 * t + 1)
                nc.gpsimd.tensor_tensor(twos[1][:, :, :], fours[:, 0:2, :], fours[:, 2:4, :], ALU.add).then_inc(pool_steps["e"], 1)
                pool.wait_ge(pool_steps["e"], r.seq("e") * 3 * TILES + 3 * t + 2)
                nc.gpsimd.tensor_tensor(ones[1][:, :], twos[1][:, 0, :], twos[1][:, 1, :], ALU.add).then_inc(pool_steps["e"], 1)
                pool.wait_ge(pool_steps["e"], r.seq("e") * 3 * TILES + 3 * t + 3)
                pool.wait_ge(read["T"], r.emptied("T", "e_bias"))
                if t == 0 and r.ran("e"):
                    pool.wait_ge(sems["stored"], r.last("stored", "e"))
                nc.gpsimd.tensor_tensor(y[:, t, :], ones[1][:, :], acc[1][:, t, :], ALU.add).then_inc(sems["y_ready"], 1)

            def body(r):
                p, a, b, d, e = (s in r.stages for s in "pabde")
                if b:
                    add_bias(r)
                if p:
                    rsqrt(r, 0, "p")
                if a:
                    combine(r, 0)
                    combine(r, 1)
                if e:
                    combine_all(r, 0)
                if a:
                    combine(r, 2)
                if e:
                    combine_all(r, 1)
                if a:
                    combine(r, 3)
                if d:
                    rsqrt(r, 2, "d")
                if a:
                    rsqrt(r, 1, "a")
                if e:
                    combine_all(r, 2)
                    combine_all(r, 3)

            def first_b():
                clear(1)
                pool.wait_ge(weights_loaded, WEIGHTS * 16)

            rounds(pool, body, {0: lambda: clear(0), 1: first_b})

        @block.tensor
        def _(pe):
            pe.wait_ge(consts_ready, NCONSTS_READY)
            pe.wait_ge(consts_loaded, 16)

            def turn(r, f, use, stage):
                pe.wait_ge(read["T"], r.claim("T", use))
                for t in range(TILES):
                    pe.wait_ge(sems[f"xn_ready{f}"], r.nth(f"xn_ready{f}", t + 1, stage))
                    last = nc.tensor.transpose(T[:, t * P:(t + 1) * P], xn[f][:, t, :], ident)
                last.then_inc(full["T"], 1)

            def gate(r):
                pe.wait_ge(read["T"], r.claim("T", "g_gate"))
                for f in range(r.ffns().start, r.ffns().stop):
                    for t in range(TILES):
                        at = (2 * t + f) * E
                        last = nc.tensor.matmul(T[:, at:at + E], xt[f][:, t * P:(t + 1) * P], wg_s[:, :], start=True, stop=True,
                                                skip_group_check=True)
                last.then_inc(full["T"], 1)

            def locations(r):
                pe.wait_ge(sems["hot_ready"], r.nth("hot_ready", 1, "g"))
                pe.wait_ge(read["T"], r.claim("T", "g_loc"))
                hb = hotb[:, :, :, :].rearrange("p t f e -> p (t f e)")
                n = 2 * E
                nc.tensor.matmul(T[:, 0:ROUTES], trib[:, :], hb, start=True, stop=False, skip_group_check=True)
                for t in range(1, TILES):
                    nc.tensor.matmul(T[:, t * n:ROUTES], onesb[:, :], hb[:, 0:ROUTES - t * n], start=False, stop=False, skip_group_check=True)
                for t in range(TILES):
                    last = nc.tensor.matmul(T[:, ROUTES:ROUTES + n], onesb[:, :], hb[:, t * n:(t + 1) * n], start=False,
                                            stop=(t == TILES - 1), skip_group_check=True)
                last.then_inc(full["T"], 1)

            def gates_turned(r):
                pe.wait_ge(sems["gm_ready"], r.nth("gm_ready", 1, "g"))
                pe.wait_ge(read["T"], r.claim("T", "g_gmt"))
                nc.tensor.transpose(T[:, 0:P], gm_all[:, :], ident).then_inc(full["T"], 1)

            def bias(r, f, stage):
                if type(r.i) is int and r.i == 0:
                    pe.wait_ge(weights_loaded, WEIGHTS * 16)
                pe.wait_ge(read["T"], r.emptied("T", "g_gmt"))
                pe.wait_ge(read["T"], r.claim("T", stage + "_bias"))
                nc.tensor.matmul(T[:, :], gmt[:, :], bexp_s[:, f, :, :].rearrange("r t c -> r (t c)"), start=True, stop=True,
                                 skip_group_check=True).then_inc(full["T"], 1)

            def experts(r, f, stage, t):
                pe.wait_ge(sems[f"xt_lo_ready{f}"], r.nth(f"xt_lo_ready{f}", 1, stage))
                hi, lo = xt_hi[f][:, t * P:(t + 1) * P], xt_lo[f][:, t * P:(t + 1) * P]
                for n in range(2):
                    out, cols = bank[f"Y{n}"][:, :], slice(n * 512, (n + 1) * 512)
                    pe.wait_ge(read[f"Y{n}"], r.claim(f"Y{n}", f"{stage}_exp{t}"))
                    nc.tensor.matmul(out, lo, we_hi[:, cols], start=True, stop=False, skip_group_check=True)
                    nc.tensor.matmul(out, hi, we_hi[:, cols], start=False, stop=False, skip_group_check=True)
                    nc.tensor.matmul(out, hi, we_lo[:, cols], start=False, stop=True, skip_group_check=True).then_inc(full[f"Y{n}"], 1)

            def q_k(r):
                pe.wait_ge(read["T"], r.emptied("T", "b_nt"))
                for n, w, use in (("Y0", wq_s, "b_q"), ("Y1", wk_s, "b_k")):
                    pe.wait_ge(read[n], r.claim(n, use))
                    nc.tensor.matmul(bank[n][:, :], w[:, :], nt[:, HALO:HALO + SEQ], start=True, stop=True,
                                     skip_group_check=True).then_inc(full[n], 1)

            def values(r):
                for n in range(2):
                    pe.wait_ge(read[f"Y{n}"], r.claim(f"Y{n}", f"b_v{n}"))
                    for m in range(4):
                        at = (4 * n + m) * W
                        last = nc.tensor.matmul(bank[f"Y{n}"][:, m * P:(m + 1) * P], nt[:, at:at + P], wv_s[:, :], start=True, stop=True,
                                                skip_group_check=True)
                    last.then_inc(full[f"Y{n}"], 1)

            def global_logits(r):
                pe.wait_ge(sems["kge_ready"], r.nth("kge_ready", 1, "b"))
                pe.wait_ge(read["T"], r.claim("T", "b_lg"))
                for t in range(TILES):
                    last = nc.tensor.matmul(T[:, t * P:(t + 1) * P], qf[:, t * P:(t + 1) * P], kge[:, :, :].rearrange("p h g -> p (h g)"),
                                            start=True, stop=True, skip_group_check=True)
                last.then_inc(full["T"], 1)

            def global_turned(r):
                pe.wait_ge(sems["pg_ready"], r.nth("pg_ready", 1, "b"))
                pe.wait_ge(read["T"], r.claim("T", "b_pgt"))
                for t in range(TILES):
                    last = nc.tensor.transpose(T[:, t * P:(t + 1) * P], pg[:, t * H:(t + 1) * H, :].rearrange("p h g -> p (h g)"), ident)
                last.then_inc(full["T"], 1)

            def global_values(r):
                pe.wait_ge(sems["xgr_ready"], r.nth("xgr_ready", 1, "b"))
                pe.wait_ge(read["T"], r.claim("T", "b_vg"))
                nc.tensor.matmul(T[:, 0:P], xgr[:, :, :].rearrange("p h g -> p (h g)"), wv_s[:, :], start=True, stop=True,
                                 skip_group_check=True).then_inc(full["T"], 1)

            def logits(r, stage, n):
                use = f"{stage}_s{n}"
                s, pb = s_bank[use], r.buf(stage)
                if n == 0 and stage == "b":
                    pe.wait_ge(sems["k_stacked"], r.nth("k_stacked", 16, "b"))
                    pe.wait_ge(sems["q_spread"], r.nth("q_spread", 4 * 16, "b"))
                if n == 0 and stage == "c":
                    pe.wait_ge(sems["max_placed0"], r.nth("max_placed0", 4 * 16, "c"))
                if n == BLOCKS // 2 and stage == "c":
                    pe.wait_ge(sems["max_placed1"], r.nth("max_placed1", 4 * 16, "c"))
                rows = STACK if stage == "b" else P
                pe.wait_ge(read[s], r.claim(s, use))
                mask = masksb[:, 1 if n == 0 else 2 if n == BLOCKS - 1 else 0, :].unsqueeze(1).broadcast_to([P, 8, W])
                for half in range(2):
                    dst = bank[s][:, half * 512:(half + 1) * 512]
                    nc.tensor.matmul(dst, identb[:, :], mask, start=True, stop=False, skip_group_check=True)
                    for c in (2 * half, 2 * half + 1):
                        last = nc.tensor.matmul(dst[:, (c % 2) * 256:(c % 2 + 1) * 256], ks[pb][0:rows, c, n * W:n * W + P],
                                                qx[pb][0:rows, c, :, n * W:(n + 1) * W], start=False, stop=True, skip_group_check=True)
                last.then_inc(full[s], 1)

            def maxima_turned(r, half):
                s = f"b_s{4 * half + 3}"
                pe.wait_ge(read[s_bank[s]], r.emptied(s_bank[s], s))
                pe.wait_ge(read["O"], r.claim("O", f"b_mt{half}"))
                nc.tensor.transpose(O[:, 0:P], rmax[:, half, :, :, :].rearrange("p h n v -> p (h n v)"), ident).then_inc(sems["max_turned"], 1)

            def weigh(r, n):
                pb = r.buf("c")
                pe.wait_ge(read[s_bank[f"c_s{n}"]], r.emptied(s_bank[f"c_s{n}"], f"c_s{n}"))
                if n % 2 == 0:
                    pe.wait_ge(read["O"], r.claim("O", f"c_o{n // 2}"))
                for h in range(H):
                    j, c = h // 4, h % 4
                    last = nc.tensor.matmul(O[32 * c:32 * c + VW, j * P + (n % 2) * W:j * P + (n % 2 + 1) * W], va[pb][:, n, h, :],
                                            pr[n % 2][:, h, :], start=True, stop=True, skip_group_check=True)
                last.then_inc(sems["weighed"], 1)

            def weighed_turned(r, t):
                pe.wait_ge(read["O"], r.emptied("O", f"c_o{t}"))
                pe.wait_ge(read["T"], r.claim("T", f"c_ot{t}"))
                for j in range(4):
                    last = nc.tensor.transpose(T[:, j * P:(j + 1) * P], osb[t % 2][:, j * P:(j + 1) * P], ident)
                last.then_inc(full["T"], 1)

            def global_out(r, t):
                pe.wait_ge(read["Y0"], r.claim("Y0", f"c_og{t}"))
                pb = r.buf("c")
                nc.tensor.matmul(Y0[:, 0:P], pgt[pb][:, t * P:(t + 1) * P], vge[pb][:, :, :].rearrange("p h d -> p (h d)"), start=True,
                                 stop=True, skip_group_check=True).then_inc(full["Y0"], 1)

            def out_turned(r, t):
                pe.wait_ge(read["Y0"], r.emptied("Y0", f"c_og{t}"))
                pe.wait_ge(read["Y1"], r.claim("Y1", f"c_bt{t}"))
                nc.tensor.transpose(Y1[:, 0:P], og[t % 2][:, :], ident).then_inc(full["Y1"], 1)

            def project(r, t):
                pe.wait_ge(read["Y1"], r.emptied("Y1", f"c_bt{t}"))
                pe.wait_ge(read["Y0"], r.claim("Y0", f"c_wo{t}"))
                nc.tensor.matmul(Y0[:, 0:P], bt[t % 2][:, :], wo_s[:, :], start=True, stop=True, skip_group_check=True)\
                    .then_inc(full["Y0"], 1)

            def body(r):
                g, a, b, c, d, e = (s in r.stages for s in "gabcde")
                if c:
                    logits(r, "c", 0)
                if e:
                    turn(r, 2, "e_xt", "e")
                if c:
                    logits(r, "c", 1)
                if b:
                    turn(r, 1, "b_nt", "b")
                if c:
                    weigh(r, 0)
                if a:
                    turn(r, 0, "a_xt", "a")
                if b:
                    q_k(r)
                if g:
                    gate(r)
                if c:
                    logits(r, "c", 2)
                if b:
                    values(r)
                if c:
                    weigh(r, 1)
                    logits(r, "c", 3)
                if b:
                    global_logits(r)
                if c:
                    weigh(r, 2)
                    logits(r, "c", 4)
                if g:
                    locations(r)
                if c:
                    weigh(r, 3)
                    logits(r, "c", 5)
                if g:
                    gates_turned(r)
                if c:
                    weigh(r, 4)
                if a:
                    bias(r, 0, "a")
                if c:
                    logits(r, "c", 6)
                if e:
                    bias(r, 1, "e")
                if c:
                    weigh(r, 5)
                    weighed_turned(r, 0)
                    logits(r, "c", 7)
                    global_out(r, 0)
                    weigh(r, 6)
                    out_turned(r, 0)
                if a:
                    experts(r, 0, "a", 0)
                if c:
                    weigh(r, 7)
                    weighed_turned(r, 1)
                    project(r, 0)
                if b:
                    logits(r, "b", 0)
                if c:
                    global_out(r, 1)
                if b:
                    logits(r, "b", 1)
                if c:
                    out_turned(r, 1)
                if a:
                    experts(r, 0, "a", 1)
                if c:
                    weighed_turned(r, 2)
                    project(r, 1)
                if b:
                    logits(r, "b", 2)
                if e:
                    experts(r, 1, "e", 0)
                if b:
                    logits(r, "b", 3)
                if c:
                    global_out(r, 2)
                if b:
                    logits(r, "b", 4)
                if c:
                    out_turned(r, 2)
                if a:
                    experts(r, 0, "a", 2)
                if c:
                    weighed_turned(r, 3)
                    project(r, 2)
                if b:
                    logits(r, "b", 5)
                if e:
                    experts(r, 1, "e", 1)
                if b:
                    maxima_turned(r, 0)
                    logits(r, "b", 6)
                if c:
                    global_out(r, 3)
                if b:
                    logits(r, "b", 7)
                if c:
                    out_turned(r, 3)
                if a:
                    experts(r, 0, "a", 3)
                if c:
                    project(r, 3)
                if b:
                    global_turned(r)
                if e:
                    experts(r, 1, "e", 2)
                if b:
                    global_values(r)
                if e:
                    experts(r, 1, "e", 3)
                if b:
                    maxima_turned(r, 1)

            def buffers(i):
                pe.wait_ge(buffers_ready[i], 4 + 2 * (i == 0))

            def weights():
                pe.wait_ge(experts_loaded, 2 * 16)
                pe.wait_ge(experts_lo_ready, 1)

            rounds(pe, body, {0: weights, 1: lambda: buffers(0), 2: lambda: buffers(1)})

        @block.scalar
        def _(act):
            act.wait_ge(consts_ready, NCONSTS_READY)

            def evacuate(r, n, use, dst, src, scale=1.0):
                act.wait_ge(full[n], r.filled(n, use))
                nc.scalar.activation(dst, src, ACT.Copy, scale=scale).then_inc(read[n], 1)

            def scale_experts(r, f, stage, t):
                done = "x1_ready" if stage == "a" else "y_ready"
                if t >= 2:
                    act.wait_ge(sems[done], r.nth(done, t - 1, stage))
                elif r.ran(stage):
                    act.wait_ge(sems[done], r.last(done, stage))
                for n in ("Y1",) if stage == "a" else ("Y0", "Y1"):
                    first = E // 2 if n == "Y1" else 0
                    act.wait_ge(full[n], r.filled(n, f"{stage}_exp{t}"))
                    for e in range(first, first + E // 2):
                        slot = e - E // 2 if stage == "a" else e
                        last = nc.scalar.activation(scaled[f][:, t % 2, slot, :], bank[n][:, (e - first) * P:(e - first + 1) * P], ACT.Copy,
                                                    scale=gms[:, t, f, e:e + 1])
                    last.then_inc(read[n], 1)

            def exp(r, n):
                use = f"c_s{n}"
                s = s_bank[use]
                act.wait_ge(full[s], r.filled(s, use))
                if n >= 2:
                    act.wait_ge(sems["weighed"], r.nth("weighed", n - 1, "c"))
                else:
                    if r.ran("c"):
                        act.wait_ge(sems["weighed"], r.last("weighed", "c"))
                nc.scalar.activation(pr[n % 2][:, :, :].rearrange("p h w -> p (h w)"), bank[s][:, :], ACT.Exp).then_inc(read[s], 1)

            def upper_tokens(r, f, stage):
                act.wait_ge(read["T"], r.emptied("T", f"{stage}_xt"))
                nc.scalar.activation(xt_hi[f][:, :], xt[f][:, :], ACT.Copy).then_inc(sems[f"xt_hi_ready{f}"], 1)

            def gate_exp(r):
                act.wait_ge(read["T"], r.emptied("T", "g_gate"))
                nc.scalar.activation(lexp[:, :, :, :], lsub[:, :, :, :], ACT.Exp).then_inc(sems["lexp_ready"], 1)

            def fp32_qk(r):
                evacuate(r, "Y0", "b_q", qf[:, :], Y0[:, :], scale=SCALE)
                evacuate(r, "Y1", "b_k", kf[:, :], Y1[:, :])

            def higher_parts(r):
                if r.ran("b"):
                    act.wait_ge(sems["q_in_dram"], r.last("q_in_dram", "b"))
                    act.wait_ge(sems["k_in_dram"], r.last("k_in_dram", "b"))
                act.wait_ge(read["Y0"], r.emptied("Y0", "b_q"))
                nc.scalar.activation(q3[:, 0:3:2, :], qf[:, :].unsqueeze(1).broadcast_to([P, 2, SEQ]), ACT.Copy).then_inc(sems["q_hi_ready"], 1)
                act.wait_ge(read["Y1"], r.emptied("Y1", "b_k"))
                nc.scalar.activation(k3[:, 0:2, HALO:HALO + SEQ], kf[:, :].unsqueeze(1).broadcast_to([P, 2, SEQ]), ACT.Copy)\
                    .then_inc(sems["k_hi_ready"], 1)

            def global_tokens(r):
                act.wait_ge(read["T"], r.emptied("T", "b_nt"))
                nc.scalar.activation(xgr[:, :, :], nt[:, HALO:HALO + SEQ:W].unsqueeze(1).broadcast_to([P, H, G]), ACT.Copy)\
                    .then_inc(sems["xgr_ready"], 1)

            def values(r):
                for n in range(2):
                    evacuate(r, f"Y{n}", f"b_v{n}", va[r.buf("b")][:, 4 * n:4 * n + 4, :, 0:DH],
                             bank[f"Y{n}"][:, :].rearrange("p (n h d) -> p n h d", n=4, h=H))

            def global_exp(r):
                act.wait_ge(read["T"], r.emptied("T", "b_lg"))
                nc.scalar.activation(lge[:, :, :], lgs[:, :, :], ACT.Exp).then_inc(sems["lge_ready"], 1)

            def pair(r, t):
                if t >= 2:
                    act.wait_ge(full["T"], r.filled("T", f"c_ot{t - 2}"))
                act.wait_ge(sems["weighed"], r.nth("weighed", 2 * t + 2, "c"))
                nc.scalar.activation(osb[t % 2][:, :], O[:, :], ACT.Copy).then_inc(read["O"], 1)

            def body(r):
                g, a, b, c, d, e = (s in r.stages for s in "gabcde")
                if c:
                    exp(r, 0)
                if e:
                    evacuate(r, "T", "e_xt", xt[1][:, :], T[:, :])
                if c:
                    exp(r, 1)
                if b:
                    evacuate(r, "T", "b_nt", nt[:, HALO:HALO + SEQ], T[:, :])
                if a:
                    evacuate(r, "T", "a_xt", xt[0][:, :], T[:, :])
                if b:
                    fp32_qk(r)
                if e:
                    upper_tokens(r, 1, "e")
                if b:
                    higher_parts(r)
                if c:
                    exp(r, 2)
                if g:
                    gate_exp(r)
                if a:
                    upper_tokens(r, 0, "a")
                if b:
                    values(r)
                if c:
                    pair(r, 0)
                    exp(r, 3)
                if b:
                    global_exp(r)
                if c:
                    exp(r, 4)
                    pair(r, 1)
                if g:
                    evacuate(r, "T", "g_gmt", gmt[:, :], T[0:ROUTES, 0:P])
                if c:
                    exp(r, 5)
                if b:
                    global_tokens(r)
                if c:
                    exp(r, 6)
                    pair(r, 2)
                    exp(r, 7)
                    evacuate(r, "Y1", "c_bt0", bt[0][:, :], Y1[:, 0:P])
                if a:
                    scale_experts(r, 0, "a", 0)
                if c:
                    pair(r, 3)
                    evacuate(r, "Y1", "c_bt1", bt[1][:, :], Y1[:, 0:P])
                if a:
                    scale_experts(r, 0, "a", 1)
                if e:
                    scale_experts(r, 1, "e", 0)
                if c:
                    evacuate(r, "Y1", "c_bt2", bt[0][:, :], Y1[:, 0:P])
                if a:
                    scale_experts(r, 0, "a", 2)
                if e:
                    scale_experts(r, 1, "e", 1)
                if c:
                    evacuate(r, "Y1", "c_bt3", bt[1][:, :], Y1[:, 0:P])
                if a:
                    scale_experts(r, 0, "a", 3)
                if b:
                    evacuate(r, "T", "b_pgt", pgt[r.buf("b")][:, :], T[:, :])
                if e:
                    scale_experts(r, 1, "e", 2)
                    scale_experts(r, 1, "e", 3)

            def buffers(i):
                act.wait_ge(buffers_ready[i], 4 + 2 * (i == 0))

            def upper_experts():
                act.wait_ge(experts_loaded, 2 * 16)
                nc.scalar.activation(we_hi[:, :], we_s[:, :], ACT.Copy, scale=WSCALE).then_inc(experts_hi_ready, 1)

            rounds(act, body, {0: upper_experts, 1: lambda: buffers(0), 2: lambda: buffers(1)})

        @block.vector
        def _(dve):
            nc.vector.memset(carry[:, :, :], 0.0).then_inc(consts_ready, 1)
            nc.vector.memset(hotb[:, :, :, :], 0.0).then_inc(consts_ready, 1)
            nc.vector.memset(lsub[:, :, :, :], 0.0).then_inc(consts_ready, 1)
            nc.vector.memset(gm_all[:, :], 0.0).then_inc(consts_ready, 1)
            for n in bank:
                nc.vector.memset(bank[n][:, :] if n == "O" else bank[n][:, 0:E], 0.0).then_inc(read[n], 1)
            dve.wait_ge(consts_loaded, 16)
            nc.vector.tensor_copy(identb[:, :], cst[:, IDENT:IDENT + P]).then_inc(consts_ready, 1)
            nc.vector.tensor_copy(trib[:, :], cst[:, TRI:TRI + P]).then_inc(consts_ready, 1)
            nc.vector.tensor_copy(onesb[:, :], cst[:, ONES:ONES + P]).then_inc(consts_ready, 1)
            nc.vector.tensor_copy(masksb[:, :, :].rearrange("p m w -> p (m w)"), cst[:, MASKS:MASKS + 3 * W]).then_inc(consts_ready, 1)
            dve.wait_ge(consts_ready, NCONSTS_READY)

            def statistics(r, f, stage, src):
                for t in range(TILES):
                    last = nc.vector.bn_stats(st[f][:, t, :], src[:, t, :])
                last.then_inc(steps[stage], 1)
                dve.wait_ge(steps[stage], r.step(stage, r.mark(stage)))
                dve.nop(nofuse=True)
                for t in range(TILES):
                    last = nc.vector.bn_aggr(mv[f][:, t, :], st[f][:, t, :])
                last.then_inc(steps[stage], 1)
                dve.wait_ge(steps[stage], r.step(stage, r.mark(stage)))
                nc.vector.tensor_scalar(ve[f][:, :], mv[f][:, :, 1], EPS, None, ALU.add).then_inc(sems[f"var_ready{f}"], 1)

            def rows(r, ap):
                return ap.rearrange("p t f e -> p (t f) e") if r.both() else ap[:, :, r.ffns().start, :]

            def columns(r, ap):
                return ap.rearrange("p t f -> p (t f)") if r.both() else ap[:, :, r.ffns().start]

            def each(r, ap):
                return columns(r, ap).unsqueeze(2).broadcast_to([P, TILES * (1 + r.both()), E])

            def tiles(r, ap):
                return ap.rearrange("p t f e -> p t (f e)") if r.both() else ap[:, :, r.ffns().start, :]

            def layernorm(r, f, stage, src):
                dve.wait_ge(sems[f"rstd_ready{f}"], r.nth(f"rstd_ready{f}", 1, stage))
                for t in range(TILES):
                    nc.vector.tensor_scalar(xn[f][:, t, :], src[:, t, :], mv[f][:, t, 0:1], rstd[f][:, t:t + 1], ALU.subtract, ALU.mult)\
                        .then_inc(sems[f"xn_ready{f}"], 1)

            def lower_tokens(r, f, stage):
                dve.wait_ge(sems[f"xt_hi_ready{f}"], r.nth(f"xt_hi_ready{f}", 1, stage))
                nc.vector.tensor_tensor(xt_lo[f][:, :], xt[f][:, :], xt_hi[f][:, :], ALU.subtract).then_inc(sems[f"xt_lo_ready{f}"], 1)

            def route(r):
                g = rows(r, T[:, 0:ROUTES].rearrange("p (t f e) -> p t f e", f=2, e=E))
                dve.wait_ge(full["T"], r.filled("T", "g_gate"))
                nc.vector.tensor_reduce(columns(r, lmax), g, AX.X, ALU.max).then_inc(steps["g"], 1)
                dve.wait_ge(steps["g"], r.step("g", r.mark("g")))
                nc.vector.tensor_tensor(rows(r, lsub), g, each(r, lmax), ALU.subtract).then_inc(read["T"], 1)

            def choose(r):
                weights = first.unsqueeze(1).broadcast_to([P, TILES * (1 + r.both()), E])
                dve.wait_ge(sems["lexp_ready"], r.nth("lexp_ready", 1, "g"))
                nc.vector.tensor_reduce(columns(r, lsum), rows(r, lexp), AX.X, ALU.add).then_inc(steps["g"], 1)
                a = r.mark("g")
                nc.vector.scalar_tensor_tensor(out=rows(r, top), in0=rows(r, lexp), scalar=1.0, in1=weights, op0=ALU.is_ge,
                                               op1=ALU.mult).then_inc(steps["g"], 1)
                b = r.mark("g")
                dve.wait_ge(steps["g"], r.step("g", a))
                nc.vector.reciprocal(columns(r, prob), columns(r, lsum))
                dve.wait_ge(steps["g"], r.step("g", b))
                nc.vector.tensor_reduce(columns(r, topm), rows(r, top), AX.X, ALU.max).then_inc(steps["g"], 1)
                dve.wait_ge(steps["g"], r.step("g", r.mark("g")))
                nc.vector.tensor_tensor(rows(r, hot), rows(r, top), each(r, topm), ALU.is_equal).then_inc(steps["g"], 1)
                dve.wait_ge(steps["g"], r.step("g", r.mark("g")))
                nc.vector.tensor_copy(rows(r, hotb), rows(r, hot)).then_inc(sems["hot_ready"], 1)

            def keep(r):
                fs = r.ffns()
                sent = carry[:, fs, :].rearrange("p f e -> p (f e)")
                counts = T[:, ROUTES + fs.start * E:ROUTES + fs.stop * E]
                dve.wait_ge(full["T"], r.filled("T", "g_loc"))
                nc.vector.tensor_tensor(tiles(r, loc), tiles(r, T[:, 0:ROUTES].rearrange("p (t f e) -> p t f e", f=2, e=E)),
                                        sent.unsqueeze(1).broadcast_to([P, TILES, E * (1 + r.both())]), ALU.add).then_inc(steps["g"], 1)
                dve.wait_ge(steps["g"], r.step("g", r.mark("g")))
                nc.vector.tensor_tensor(sent, sent, counts, ALU.add).then_inc(read["T"], 1)
                nc.vector.scalar_tensor_tensor(out=rows(r, top), in0=rows(r, loc), scalar=float(CAP), in1=rows(r, hot),
                                               op0=ALU.is_lt, op1=ALU.mult).then_inc(steps["g"], 1)
                dve.wait_ge(steps["g"], r.step("g", r.mark("g")))
                nc.vector.scalar_tensor_tensor(out=rows(r, gms), in0=rows(r, top), scalar=0.5 / WSCALE, in1=each(r, prob),
                                               op0=ALU.mult, op1=ALU.mult)
                nc.vector.scalar_tensor_tensor(out=rows(r, gm), in0=rows(r, top), scalar=0.5, in1=each(r, prob),
                                               op0=ALU.mult, op1=ALU.mult).then_inc(sems["gm_ready"], 1)

            def residual(r, f, stage, src):
                if stage == "e" and r.ran("e"):
                    dve.wait_ge(sems["y_ready"], r.last("y_ready", "e"))
                dve.wait_ge(full["T"], r.filled("T", f"{stage}_bias"))
                nc.vector.tensor_tensor(acc[f][:, :, :], T[:, :].rearrange("p (t c) -> p t c", t=TILES), src[:, :, :], ALU.add)\
                    .then_inc(read["T"], 1)

            def combine(r, t):
                dve.wait_ge(read["T"], r.emptied("T", "a_bias"))
                dve.wait_ge(full["Y0"], r.filled("Y0", f"a_exp{t}"))
                marks = {}
                for e in range(E // 2):
                    src = Y0[:, e * P:(e + 1) * P]
                    if e >= 2:
                        dve.wait_ge(steps["a"], r.step("a", marks[e - 2]))
                    if e == 1:
                        ins = nc.vector.tensor_scalar(odd[0][:, t, :], src, gms[:, t, 0, e:e + 1], None, ALU.mult)
                    else:
                        half = odd[0] if e % 2 else acc[0]
                        ins = nc.vector.scalar_tensor_tensor(out=half[:, t, :], in0=src, scalar=gms[:, t, 0, e:e + 1], in1=half[:, t, :],
                                                             op0=ALU.mult, op1=ALU.add)
                    if e == E // 2 - 1:
                        ins.then_inc(read["Y0"], 1)
                    else:
                        ins.then_inc(steps["a"], 1)
                        marks[e] = r.mark("a")
                dve.wait_ge(steps["a"], r.step("a", marks[2]))
                dve.wait_ge(read["Y0"], r.emptied("Y0", f"a_exp{t}"))
                nc.vector.tensor_tensor(acc[0][:, t, :], acc[0][:, t, :], odd[0][:, t, :], ALU.add).then_inc(sems["first_four_ready"], 1)

            def lower_parts(r):
                dve.wait_ge(sems["q_hi_ready"], r.nth("q_hi_ready", 1, "b"))
                nc.vector.tensor_tensor(q3[:, 1, :], qf[:, :], q3[:, 0, :], ALU.subtract).then_inc(sems["q_lo_ready"], 1)
                dve.wait_ge(sems["k_hi_ready"], r.nth("k_hi_ready", 1, "b"))
                nc.vector.tensor_tensor(k3[:, 2, HALO:HALO + SEQ], kf[:, :], k3[:, 0, HALO:HALO + SEQ], ALU.subtract)\
                    .then_inc(sems["k_lo_ready"], 1)
                nc.vector.tensor_tensor(kge[:, :, :], heads.unsqueeze(2).broadcast_to([P, H, G]),
                                        kf[:, ::W].unsqueeze(1).broadcast_to([P, H, G]), ALU.mult).then_inc(sems["kge_ready"], 1)

            def all_g(ap):
                return ap.unsqueeze(2).broadcast_to([P, TILES * H, G])

            def global_shift(r):
                lg = T[:, :].rearrange("p (th g) -> p th g", g=G)
                dve.wait_ge(full["T"], r.filled("T", "b_lg"))
                nc.vector.tensor_reduce(lgm[:, :], lg, AX.X, ALU.max).then_inc(steps["b"], 1)
                dve.wait_ge(steps["b"], r.step("b", r.mark("b")))
                nc.vector.tensor_tensor(lgs[:, :, :], lg, all_g(lgm[:, :]), ALU.subtract).then_inc(read["T"], 1)

            def global_probs(r):
                dve.wait_ge(sems["lge_ready"], r.nth("lge_ready", 1, "b"))
                nc.vector.tensor_reduce(lgr[:, :], lge[:, :, :], AX.X, ALU.add).then_inc(steps["b"], 1)
                dve.wait_ge(steps["b"], r.step("b", r.mark("b")))
                nc.vector.reciprocal(lgi[:, :], lgr[:, :]).then_inc(steps["b"], 1)
                dve.wait_ge(steps["b"], r.step("b", r.mark("b")))
                nc.vector.tensor_tensor(pg[:, :, :], lge[:, :, :], all_g(lgi[:, :]), ALU.mult).then_inc(sems["pg_ready"], 1)

            def global_values(r):
                dve.wait_ge(full["T"], r.filled("T", "b_vg"))
                nc.vector.tensor_tensor(vge[r.buf("b")][:, :, :], T[:, 0:P].rearrange("p (h d) -> p h d", d=DH),
                                        heads.unsqueeze(2).broadcast_to([P, H, DH]), ALU.mult).then_inc(read["T"], 1)

            def block_max(r, n):
                use = f"b_s{n}"
                s = s_bank[use]
                dve.wait_ge(full[s], r.filled(s, use))
                nc.vector.tensor_reduce(rmax[:, n // 4, :, n % 4, :], bank[s][:, :].rearrange("p (h v q) -> p h v q", v=2, q=32), AX.X,
                                        ALU.max, apply_transpose=True).then_inc(read[s], 1)

            def query_max(r, half):
                dve.wait_ge(sems["max_turned"], r.nth("max_turned", half + 1, "b"))
                nc.vector.tensor_reduce(nmax[:, half, :], O[:, 0:P].rearrange("p (k q) -> p q k", k=4), AX.X, ALU.max, negate=True)\
                    .then_inc(read["O"], 1)

            def normalise(r, t):
                dve.wait_ge(full["T"], r.filled("T", f"c_ot{t}"))
                o = T[:, :].rearrange("p (h u) -> p h u", u=32)
                nc.vector.reciprocal(rl[t % 2][:, :], o[:, :, DH]).then_inc(steps["c"], 1)
                dve.wait_ge(steps["c"], r.step("c", r.mark("c")))
                nc.vector.tensor_tensor(ol[t % 2][:, :, :], o[:, :, 0:DH], rl[t % 2][:, :].unsqueeze(2).broadcast_to([P, H, DH]), ALU.mult)\
                    .then_inc(read["T"], 1)

            def add_global(r, t):
                dve.wait_ge(full["Y0"], r.filled("Y0", f"c_og{t}"))
                dve.wait_ge(read["T"], r.emptied("T", f"c_ot{t}"))
                nc.vector.tensor_tensor(og[t % 2][:, :], ol[t % 2][:, :, :].rearrange("p h d -> p (h d)"), Y0[:, 0:P], ALU.add)\
                    .then_inc(read["Y0"], 1)

            def attention_out(r, t):
                if t == 0 and "e" in r.stages:
                    dve.wait_ge(read["T"], r.emptied("T", "e_bias"))
                dve.wait_ge(full["Y0"], r.filled("Y0", f"c_wo{t}"))
                nc.vector.tensor_tensor(x2[:, t, :], Y0[:, 0:P], x1b[r.buf("c")][:, t, :], ALU.add).then_inc(read["Y0"], 1)

            def statistics_x(r):
                dve.wait_ge(sems["x_loaded"], r.nth("x_loaded", 16, "p"))
                statistics(r, 0, "p", x0[r.buf("p")])

            def statistics_x1(r):
                dve.wait_ge(sems["x1_ready"], r.nth("x1_ready", TILES, "a"))
                statistics(r, 1, "a", x1[r.buf("a")])

            def statistics_x2(r):
                dve.wait_ge(read["Y0"], r.emptied("Y0", "c_wo3"))
                statistics(r, 2, "d", x2)

            def body(r):
                p, g, a, b, c, d, e = (s in r.stages for s in "pgabcde")
                if b:
                    lower_parts(r)
                if g:
                    route(r)
                    choose(r)
                if a:
                    lower_tokens(r, 0, "a")
                if e:
                    lower_tokens(r, 1, "e")
                if b:
                    global_shift(r)
                if g:
                    keep(r)
                if p:
                    statistics_x(r)
                if a:
                    residual(r, 0, "a", x0[r.buf("a")])
                if e:
                    residual(r, 1, "e", x2)
                if b:
                    global_probs(r)
                if c:
                    normalise(r, 0)
                    add_global(r, 0)
                if p:
                    layernorm(r, 0, "p", x0[r.buf("p")])
                if a:
                    combine(r, 0)
                if c:
                    normalise(r, 1)
                    attention_out(r, 0)
                    add_global(r, 1)
                if b:
                    block_max(r, 0)
                if a:
                    combine(r, 1)
                if c:
                    normalise(r, 2)
                    attention_out(r, 1)
                if b:
                    block_max(r, 1)
                    block_max(r, 2)
                if c:
                    add_global(r, 2)
                if b:
                    block_max(r, 3)
                if a:
                    combine(r, 2)
                if c:
                    normalise(r, 3)
                    attention_out(r, 2)
                if b:
                    block_max(r, 4)
                    block_max(r, 5)
                if c:
                    add_global(r, 3)
                if b:
                    query_max(r, 0)
                    block_max(r, 6)
                if a:
                    combine(r, 3)
                if c:
                    attention_out(r, 3)
                if d:
                    statistics_x2(r)
                if b:
                    block_max(r, 7)
                if a:
                    statistics_x1(r)
                if d:
                    layernorm(r, 2, "d", x2)
                if b:
                    global_values(r)
                if a:
                    layernorm(r, 1, "a", x1[r.buf("a")])
                if b:
                    query_max(r, 1)
                for s, n in DVE_STEPS.items():
                    assert s not in r.stages or r.steps[s] == n, (s, r.steps[s])

            def buffers(i):
                dve.wait_ge(buffers_ready[i], 4 + 2 * (i == 0))

            def lower_experts():
                dve.wait_ge(experts_loaded, 2 * 16)
                dve.wait_ge(experts_hi_ready, 1)
                nc.vector.scalar_tensor_tensor(out=we_lo[:, :], in0=we_s[:, :], scalar=WSCALE, in1=we_hi[:, :], op0=ALU.mult,
                                               op1=ALU.subtract).then_inc(experts_lo_ready, 1)

            rounds(dve, body, {0: lower_experts, 1: lambda: buffers(0), 2: lambda: buffers(1)})


DVE_STEPS = {"p": 2, "g": 7, "a": 14, "b": 3, "c": 4, "d": 2}
NCONSTS_READY = 9
WEIGHTS = 5 + 2 * TILES


def constants(np):
    c = np.zeros((P, NCONST), np.float32)
    k = np.arange(P)[:, None]
    c[:, IDENT:IDENT + P] = np.eye(P)
    c[:, TRI:TRI + P] = k < np.arange(P)[None]
    c[:, ONES:ONES + P] = 1.0
    band = (k >= np.arange(W)[None]) & (k - np.arange(W)[None] <= W - 1)
    inside = [k >= 0, k >= HALO, k < P - HALO]
    for m in range(3):
        c[:, MASKS + m * W:MASKS + (m + 1) * W] = np.where(band & inside[m], 0.0, NEG)
    c[:, HEADS:HEADS + H] = k // DH == np.arange(H)[None]
    c[:, FIRST:FIRST + E] = E - np.arange(E)
    return c


def kernel(**inputs):
    import numpy as np
    import concourse.bacc as bacc
    from concourse.bass_utils import run_bass_kernel_spmd

    a = {k: np.asarray(v) for k, v in inputs.items()}
    w_qkv = a["L0_attn_w_qkv"]
    arrays = {
        "x": a["L0_attn_x"],
        "w_q": w_qkv[:, 0:P], "w_k": w_qkv[:, P:2 * P], "w_v": w_qkv[:, 2 * P:3 * P],
        "w_out": a["L0_attn_w_out"],
        "b_out": np.broadcast_to(a["L0_attn_b_out"], (P, P)),
        "w_gate": a["L0_ffn_wg"],
        "w_exp": a["L0_ffn_W"].transpose(2, 0, 1).reshape(P, E * P),
        "b_exp": a["L0_ffn_b"],
        "const": constants(np),
    }
    nc = bacc.Bacc("TRN2", target_bir_lowering=False, num_devices=1)
    arrays = {f"in_{n}": np.ascontiguousarray(v) for n, v in arrays.items()}
    aps = [nc.dram_tensor(n, v.shape, mybir.dt.from_np(v.dtype), kind="ExternalInput").ap() for n, v in arrays.items()]
    out = nc.dram_tensor("out", (NB, SEQ, P), F32, kind="ExternalOutput").ap()
    build(nc, *aps, out)
    r = run_bass_kernel_spmd(nc, [arrays], core_ids=[0])
    return r.results[0]["out"]
```
